# Optimizing a Trainium2 kernel written in Bass

```python
import numpy as np
import jax
import jax.numpy as jnp

def _softmax(x, axis=-1):
    return jax.nn.softmax(x, axis=axis)

def _gelu(x):
    return jax.nn.gelu(x, approximate=True)

def _silu(x):
    return jax.nn.silu(x)

def _sigmoid(x):
    return jax.nn.sigmoid(x)

def _layernorm(x, axis=-1, eps=1e-05):
    m = jnp.mean(x, axis=axis, keepdims=True)
    v = jnp.var(x, axis=axis, keepdims=True)
    return (x - m) / jnp.sqrt(v + eps)

def _scatter_add(tgt, idx, src, axis=0):
    return tgt.at[idx].add(src)

def _segment_sum(src, seg, n):
    return jax.ops.segment_sum(src, seg, n)
kernel_name = 'mk_flamingo_gated_d2_seqx_r8_4fc3f5'

def setup_inputs(seed: int=0):
    np.random.seed(seed)
    _w = jnp.asarray

    def _rec_inputs():
        import jax
        import jax.numpy as jnp
        _rk = jax.random.key(seed)
        x = 7.22e-05 + 1 * jax.random.normal(jax.random.fold_in(_rk, 1), (16, 128, 128), jnp.float32)
        _lenS = 128 - jax.random.randint(jax.random.fold_in(_rk, 7), (16,), 0, max(1, 128 // 4) + 1, jnp.int32)
        _lenS2 = 120 - jax.random.randint(jax.random.fold_in(_rk, 8), (16,), 0, max(1, 120 // 4) + 1, jnp.int32)
        _ctx_1024P = jax.random.normal(jax.random.fold_in(_rk, 11), (16, 16, 128), jnp.float32)
        _ctx_1024c = jax.random.dirichlet(jax.random.fold_in(_rk, 511), 0.3 * jnp.ones((16,), jnp.float32), (16, 120))
        _ctx_1024t = jnp.einsum('bsk,bkd->bsd', _ctx_1024c, _ctx_1024P)
        _ctx_1024t = _ctx_1024t * jax.lax.rsqrt(jnp.mean(jnp.square(_ctx_1024t)) + 1e-12) * 0.953939
        ctx_1024 = 4.13588e-05 + 0.999923 * (_ctx_1024t + 0.3 * jax.random.normal(jax.random.fold_in(_rk, 611), (16, 120, 128), jnp.float32))
        _g = jax.random.normal(jax.random.fold_in(_rk, 9001), (2, 2), jnp.float32)
        _g = jnp.sign(_g) * jnp.maximum(jnp.abs(_g), 1.0) + (_g == 0) * 1.0
        g_xattn = _g[0]
        g_ffn = _g[1]
        return (x, ctx_1024, g_xattn, g_ffn)
    x, ctx_1024, g_xattn, g_ffn = _rec_inputs()

    def _L0_xattn_setup():
        import jax, jax.numpy as jnp
        import numpy as np
        DIM = 128
        HEADS = 16
        HEAD_DIM = DIM // HEADS
        key = jax.random.key(seed)
        ks = jax.random.split(key, 10)
        B, N, M = (4, 256, 256)
        s = 1.0 / np.sqrt(DIM)
        return {'x': jax.random.normal(ks[0], (B, N, DIM), jnp.float32), 'context': jax.random.normal(ks[1], (B, M, DIM), jnp.float32), 'Wq': jax.random.normal(ks[2], (DIM, DIM), jnp.float32) * s, 'bq': jnp.zeros((DIM,), jnp.float32), 'Wk': jax.random.normal(ks[3], (DIM, DIM), jnp.float32) * s, 'bk': jnp.zeros((DIM,), jnp.float32), 'Wv': jax.random.normal(ks[4], (DIM, DIM), jnp.float32) * s, 'bv': jnp.zeros((DIM,), jnp.float32), 'Wo': jax.random.normal(ks[5], (DIM, DIM), jnp.float32) * s, 'bo': jnp.zeros((DIM,), jnp.float32)}
    _L0_xattn_all = _L0_xattn_setup()
    _L0_xattn_in = {k: v for k, v in _L0_xattn_all.items() if k in ('Wq', 'bq', 'Wk', 'bk', 'Wv', 'bv', 'Wo', 'bo')}
    del _L0_xattn_all

    def _L0_ffn_setup():
        import jax, jax.numpy as jnp
        import numpy as np
        H = 128
        I = 128
        E = 16
        K = 4
        LIMIT = 7.0
        ALPHA = 1.702
        EPS = 1e-05
        key = jax.random.key(seed)
        ks = jax.random.split(key, 8)
        x = jax.random.normal(ks[0], (2, 64, H), dtype=jnp.float32)
        norm_scale = jnp.ones((H,), dtype=jnp.float32)
        wg = jax.random.normal(ks[1], (H, E), dtype=jnp.float32) * 0.02
        bg = jax.random.normal(ks[2], (E,), dtype=jnp.float32) * 0.02
        w1 = jax.random.normal(ks[3], (E, H, 2 * I), dtype=jnp.float32) * 0.02
        b1 = jax.random.normal(ks[4], (E, 2 * I), dtype=jnp.float32) * 0.02
        w2 = jax.random.normal(ks[5], (E, I, H), dtype=jnp.float32) * 0.02
        b2 = jax.random.normal(ks[6], (E, H), dtype=jnp.float32) * 0.02
        return {'x': x, 'norm_scale': norm_scale, 'wg': wg, 'bg': bg, 'w1': w1, 'b1': b1, 'w2': w2, 'b2': b2}
    _L0_ffn_all = _L0_ffn_setup()
    _L0_ffn_in = {k: v for k, v in _L0_ffn_all.items() if k in ('norm_scale', 'wg', 'bg', 'w1', 'b1', 'w2', 'b2')}
    del _L0_ffn_all

    def _L1_xattn_setup():
        import jax, jax.numpy as jnp
        import numpy as np
        D = 128
        key = jax.random.key(seed)
        ks = jax.random.split(key, 9)
        B, Nq, Nk = (8, 256, 256)
        s = 1.0 / np.sqrt(D)
        return {'query': jax.random.normal(ks[0], (B, Nq, D), jnp.float32), 'key': jax.random.normal(ks[1], (B, Nk, D), jnp.float32), 'value': jax.random.normal(ks[2], (B, Nk, D), jnp.float32), 'Wq': jax.random.uniform(ks[3], (D, D), jnp.float32, -s, s), 'bq': jax.random.uniform(ks[4], (D,), jnp.float32, -s, s), 'Wk': jax.random.uniform(ks[5], (D, D), jnp.float32, -s, s), 'bk': jax.random.uniform(ks[6], (D,), jnp.float32, -s, s), 'Wv': jax.random.uniform(ks[7], (D, D), jnp.float32, -s, s), 'bv': jax.random.uniform(ks[8], (D,), jnp.float32, -s, s)}
    _L1_xattn_all = _L1_xattn_setup()
    _L1_xattn_in = {k: v for k, v in _L1_xattn_all.items() if k in ('Wq', 'bq', 'Wk', 'bk', 'Wv', 'bv')}
    del _L1_xattn_all

    def _L1_ffn_setup():
        import jax, jax.numpy as jnp
        import numpy as np
        D_MODEL = 128
        EXPANSION = 4
        D_HIDDEN = D_MODEL * EXPANSION
        NUM_STAGES = int(np.log2(D_HIDDEN))

        def butterfly(y, weights, dim):
            lead = y.shape[:-1]
            for stage in range(weights.shape[0]):
                s = 2 ** stage
                nb = dim // (2 * s)
                yr = y.reshape(*lead, nb, 2, s)
                a = yr[..., 0, :]
                b = yr[..., 1, :]
                w = weights[stage].reshape(nb, s, 2, 2)
                na = w[..., 0, 0] * a + w[..., 0, 1] * b
                nb2 = w[..., 1, 0] * a + w[..., 1, 1] * b
                y = jnp.stack([na, nb2], axis=-2).reshape(*lead, dim)
            return y
        key = jax.random.key(seed)
        ks = jax.random.split(key, 6)
        B, S = (4, 256)
        x = jax.random.normal(ks[0], (B, S, D_MODEL), jnp.float32)
        W_exp = jax.random.normal(ks[1], (D_MODEL, D_HIDDEN), jnp.float32) * 0.02
        b_exp = jnp.zeros((D_HIDDEN,), jnp.float32)
        up_weights = jax.random.normal(ks[2], (NUM_STAGES, D_HIDDEN // 2, 2, 2), jnp.float32) * 0.02
        up_bias = jnp.zeros((D_HIDDEN,), jnp.float32)
        down_weights = jax.random.normal(ks[3], (NUM_STAGES, D_HIDDEN // 2, 2, 2), jnp.float32) * 0.02
        W_con = jax.random.normal(ks[4], (D_HIDDEN, D_MODEL), jnp.float32) * 0.02
        b_con = jnp.zeros((D_MODEL,), jnp.float32)
        down_bias = jnp.zeros((D_MODEL,), jnp.float32)
        return dict(x=x, W_exp=W_exp, b_exp=b_exp, up_weights=up_weights, up_bias=up_bias, down_weights=down_weights, W_con=W_con, b_con=b_con, down_bias=down_bias)
    _L1_ffn_all = _L1_ffn_setup()
    _L1_ffn_in = {k: v for k, v in _L1_ffn_all.items() if k in ('W_exp', 'b_exp', 'up_weights', 'up_bias', 'down_weights', 'W_con', 'b_con', 'down_bias')}
    del _L1_ffn_all
    return {'x': x, 'ctx_1024': ctx_1024, 'g_xattn': g_xattn, 'g_ffn': g_ffn, 'L0_xattn_Wq': _L0_xattn_in['Wq'], 'L0_xattn_bq': _L0_xattn_in['bq'], 'L0_xattn_Wk': _L0_xattn_in['Wk'], 'L0_xattn_bk': _L0_xattn_in['bk'], 'L0_xattn_Wv': _L0_xattn_in['Wv'], 'L0_xattn_bv': _L0_xattn_in['bv'], 'L0_xattn_Wo': _L0_xattn_in['Wo'], 'L0_xattn_bo': _L0_xattn_in['bo'], 'L0_ffn_norm_scale': _L0_ffn_in['norm_scale'], 'L0_ffn_wg': _L0_ffn_in['wg'], 'L0_ffn_bg': _L0_ffn_in['bg'], 'L0_ffn_w1': _L0_ffn_in['w1'], 'L0_ffn_b1': _L0_ffn_in['b1'], 'L0_ffn_w2': _L0_ffn_in['w2'], 'L0_ffn_b2': _L0_ffn_in['b2'], 'L1_xattn_Wq': _L1_xattn_in['Wq'], 'L1_xattn_bq': _L1_xattn_in['bq'], 'L1_xattn_Wk': _L1_xattn_in['Wk'], 'L1_xattn_bk': _L1_xattn_in['bk'], 'L1_xattn_Wv': _L1_xattn_in['Wv'], 'L1_xattn_bv': _L1_xattn_in['bv'], 'L1_ffn_W_exp': _L1_ffn_in['W_exp'], 'L1_ffn_b_exp': _L1_ffn_in['b_exp'], 'L1_ffn_up_weights': _L1_ffn_in['up_weights'], 'L1_ffn_up_bias': _L1_ffn_in['up_bias'], 'L1_ffn_down_weights': _L1_ffn_in['down_weights'], 'L1_ffn_W_con': _L1_ffn_in['W_con'], 'L1_ffn_b_con': _L1_ffn_in['b_con'], 'L1_ffn_down_bias': _L1_ffn_in['down_bias']}

def reference(x, ctx_1024, g_xattn, g_ffn, L0_xattn_Wq, L0_xattn_bq, L0_xattn_Wk, L0_xattn_bk, L0_xattn_Wv, L0_xattn_bv, L0_xattn_Wo, L0_xattn_bo, L0_ffn_norm_scale, L0_ffn_wg, L0_ffn_bg, L0_ffn_w1, L0_ffn_b1, L0_ffn_w2, L0_ffn_b2, L1_xattn_Wq, L1_xattn_bq, L1_xattn_Wk, L1_xattn_bk, L1_xattn_Wv, L1_xattn_bv, L1_ffn_W_exp, L1_ffn_b_exp, L1_ffn_up_weights, L1_ffn_up_bias, L1_ffn_down_weights, L1_ffn_W_con, L1_ffn_b_con, L1_ffn_down_bias):
    import jax
    import jax.numpy as jnp

    def _L0_xattn_ref(x, context, Wq, bq, Wk, bk, Wv, bv, Wo, bo):
        import jax, jax.numpy as jnp
        import numpy as np
        DIM = 128
        HEADS = 16
        HEAD_DIM = DIM // HEADS
        B, N, C = x.shape
        M = context.shape[1]
        scale = HEAD_DIM ** (-0.5)
        q = (x @ Wq.T + bq).reshape(B, N, HEADS, HEAD_DIM).transpose(0, 2, 1, 3)
        k = (context @ Wk.T + bk).reshape(B, M, HEADS, HEAD_DIM).transpose(0, 2, 1, 3)
        v = (context @ Wv.T + bv).reshape(B, M, HEADS, HEAD_DIM).transpose(0, 2, 1, 3)
        attn = jax.nn.softmax(jnp.einsum('bhnd,bhmd->bhnm', q, k) * scale, axis=-1)
        out = jnp.einsum('bhnm,bhmd->bhnd', attn, v)
        out = out.transpose(0, 2, 1, 3).reshape(B, N, C)
        return out @ Wo.T + bo

    def _L0_ffn_ref(x, norm_scale, wg, bg, w1, b1, w2, b2):
        import jax, jax.numpy as jnp
        import numpy as np
        H = 128
        I = 128
        E = 16
        K = 4
        LIMIT = 7.0
        ALPHA = 1.702
        EPS = 1e-05
        shape = x.shape
        xf = x.reshape(-1, shape[-1])
        xn = xf * jax.lax.rsqrt(jnp.mean(xf * xf, axis=-1, keepdims=True) + EPS) * norm_scale
        logits = xn @ wg + bg
        vals, idx = jax.lax.top_k(logits, K)
        gates = jax.nn.softmax(vals, axis=-1)
        gate_full = jnp.einsum('tke,tk->te', jax.nn.one_hot(idx, E, dtype=gates.dtype), gates)
        h = jnp.einsum('th,ehd->etd', xn, w1) + b1[:, None, :]
        a = jnp.minimum(h[..., ::2], LIMIT)
        b = jnp.clip(h[..., 1::2], -LIMIT, LIMIT)
        s = a * jax.nn.sigmoid(ALPHA * a) * (b + 1.0)
        y = jnp.einsum('eti,eih->eth', s, w2) + b2[:, None, :]
        t = jnp.einsum('eth,te->th', y, gate_full)
        return x + t.reshape(shape)

    def _L1_xattn_ref(query, key, value, Wq, bq, Wk, bk, Wv, bv):
        import jax, jax.numpy as jnp
        import numpy as np
        D = 128
        q = jnp.einsum('bnd,ed->bne', query, Wq) + bq
        k = jnp.einsum('bnd,ed->bne', key, Wk) + bk
        v = jnp.einsum('bnd,ed->bne', value, Wv) + bv
        scores = jnp.einsum('bqd,bkd->bqk', q, k)
        attn = jax.nn.softmax(scores, axis=-1)
        return jnp.einsum('bqk,bkd->bqd', attn, v)

    def _L1_ffn_ref(x, W_exp, b_exp, up_weights, up_bias, down_weights, W_con, b_con, down_bias):
        import jax, jax.numpy as jnp
        import numpy as np
        D_MODEL = 128
        EXPANSION = 4
        D_HIDDEN = D_MODEL * EXPANSION
        NUM_STAGES = int(np.log2(D_HIDDEN))

        def butterfly(y, weights, dim):
            lead = y.shape[:-1]
            for stage in range(weights.shape[0]):
                s = 2 ** stage
                nb = dim // (2 * s)
                yr = y.reshape(*lead, nb, 2, s)
                a = yr[..., 0, :]
                b = yr[..., 1, :]
                w = weights[stage].reshape(nb, s, 2, 2)
                na = w[..., 0, 0] * a + w[..., 0, 1] * b
                nb2 = w[..., 1, 0] * a + w[..., 1, 1] * b
                y = jnp.stack([na, nb2], axis=-2).reshape(*lead, dim)
            return y
        h = jnp.einsum('bsd,dh->bsh', x, W_exp) + b_exp
        h = butterfly(h, up_weights, D_HIDDEN)
        h = jax.nn.gelu(h + up_bias, approximate=False)
        h = butterfly(h, down_weights, D_HIDDEN)
        y = jnp.einsum('bsh,hd->bsd', h, W_con) + b_con
        return y + down_bias
    x = x + jnp.tanh(g_xattn[0]) * _L0_xattn_ref(_layernorm(x, axis=-1), ctx_1024, L0_xattn_Wq, L0_xattn_bq, L0_xattn_Wk, L0_xattn_bk, L0_xattn_Wv, L0_xattn_bv, L0_xattn_Wo, L0_xattn_bo)
    x = x + jnp.tanh(g_ffn[0]) * _L0_ffn_ref(_layernorm(x, axis=-1), L0_ffn_norm_scale, L0_ffn_wg, L0_ffn_bg, L0_ffn_w1, L0_ffn_b1, L0_ffn_w2, L0_ffn_b2)
    x = x + jnp.tanh(g_xattn[1]) * _L1_xattn_ref(_layernorm(x, axis=-1), ctx_1024, ctx_1024, L1_xattn_Wq, L1_xattn_bq, L1_xattn_Wk, L1_xattn_bk, L1_xattn_Wv, L1_xattn_bv)
    x = x + jnp.tanh(g_ffn[1]) * _L1_ffn_ref(_layernorm(x, axis=-1), L1_ffn_W_exp, L1_ffn_b_exp, L1_ffn_up_weights, L1_ffn_up_bias, L1_ffn_down_weights, L1_ffn_W_con, L1_ffn_b_con, L1_ffn_down_bias)
    return x

_drawn_inputs = setup_inputs


def setup_inputs(seed=0):
    import zlib

    import numpy as np

    out = dict(_drawn_inputs(seed))
    spreads = {'g_ffn': (-1.0, 0.6),
     'L0_xattn_bq': (0.0, 0.324),
     'L0_xattn_bk': (0.0, 0.8),
     'L0_xattn_bv': (0.0, 0.1),
     'L0_xattn_bo': (0.0, 0.1),
     'L0_ffn_norm_scale': (1.0, 0.6),
     'L1_ffn_b_exp': (0.0, 0.1),
     'L1_ffn_up_bias': (0.0, 0.1),
     'L1_ffn_b_con': (0.0, 0.1),
     'L1_ffn_down_bias': (0.0, 0.1)}
    factors = {'L0_ffn_bg': 4.903, 'L0_ffn_b1': 8.0, 'L1_xattn_bk': 8.0}
    for name, (base, spread) in spreads.items():
        noise = np.random.default_rng([zlib.crc32(name.encode()), seed]).standard_normal(out[name].shape)
        drawn = base * np.exp(spread * noise) if base else spread * noise
        out[name] = jnp.asarray(drawn.astype(out[name].dtype))
    for name, factor in factors.items():
        out[name] = (out[name] * factor).astype(out[name].dtype)
    return out
```

```python
from contextlib import ExitStack

import numpy as np

import concourse.bass as bass
from concourse import mybir

F32 = mybir.dt.float32
F32R = mybir.dt.float32r
ALU = mybir.AluOpType
ACT = mybir.ActivationFunctionType
AX = mybir.AxisListType

P = 128
GB = 4
C3 = 3
LIMIT = 7.0
ALPHA = 1.702
EPS = 1e-5
SIG_LIMIT = float(1.0 / (1.0 + np.exp(-ALPHA * LIMIT)))


class Own:

    def __init__(self, eng, sem):
        self.eng, self.sem, self.n, self.base = eng, sem, 0, 0

    def then_wait(self, ins):
        ins.then_inc(self.sem, 1)
        self.n += 1
        self.eng.wait_ge(self.sem, self.base + self.n)

    def mark(self, ins):
        ins.then_inc(self.sem, 1)
        self.n += 1

    def wait(self):
        self.eng.wait_ge(self.sem, self.base + self.n)


def flamingo_layers(nc, a, out):
    NB, NT, D = a["x"].shape
    M = a["ctx_1024"].shape[1]
    E = a["L0_ffn_wg"].shape[1]
    HD = 8
    H = D // HD
    HG = 4
    HR = H // HG
    G = NB // GB
    GT = GB * NT
    HID = a["L1_ffn_W_exp"].shape[1]
    HC = HID // P
    STAGES = a["L1_ffn_up_weights"].shape[0]
    SCALE = HD ** -0.5
    assert NT == P and D == P and H == HG * HR

    with ExitStack() as ctx:
        def sb(name, shape, dt=F32):
            return ctx.enter_context(nc.sbuf_tensor(name, shape, dt))

        def sem(name):
            return ctx.enter_context(nc.semaphore(name))

        x_sb = sb("x_sb", [P, NB, D])
        xr = sb("xr", [P, NB, D])
        v1_all = sb("v1_all", [M, NB, D])
        k1_all = sb("k1_all", [P, NB * M])
        w1_hi = sb("w1_hi", [P, E, 2, P], F32R)
        w1_lo = sb("w1_lo", [P, E, 2, P], F32R)
        w2_sb = x_sb
        stats = sb("stats", [P, NB, 6])
        mean = sb("mean", [P, NB])
        rstd = sb("rstd", [P, NB])
        rms = sb("rms", [P, NB])
        st = sb("st", [P, 6, NB])
        rings = sb("rings", [P, 7, 2, GT])
        ident = sb("ident", [P, P])
        ones_raw = rings[:, 2, 0, :].rearrange("p (r m) -> p r m", r=HR)
        pick = sb("pick", [P, HR, P], F32R)
        pick_e_raw = rings[0:32, 0:2, :, :].rearrange("p a b (c m) -> p (a b c) m", m=P)
        pick_e = sb("pick_e", [32, E, P], F32R)
        nmask_q = sb("nmask_q", [P, 1])
        nmask_k = sb("nmask_k", [P, 1])
        mrow = sb("mrow", [1, 2, P])
        NW = 7
        wnat = sb("wnat", [P, NW, P])
        wt = sb("wt", [P, NW, P])
        WQ0, WK0, WV0, WO0, WQ1, WK1, WV1 = range(NW)
        wq_st = sb("wq_st", [P, HR, HG, 32])
        wk_st = sb("wk_st", [P, HR, HG, 32])
        brow = sb("brow", [1, 2, P])
        bst = rings[0:1, 3, :, :]
        bst_hi = sb("bst_hi", [1, 2, H * 32], F32R)
        bst_lo = sb("bst_lo", [1, 2, H * 32], F32R)
        bq_rows = sb("bq_rows", [2 * HR, P], F32R)
        bk_rows = sb("bk_rows", [2 * HR, P], F32R)
        bcast = sb("bcast", [P, 5, D])
        BV0, BO, BV1, BC, BD = range(5)
        bcol = sb("bcol", [P, 3])
        tg = sb("tg", [P, 4])
        graw = sb("graw", [P, 4])
        wg_sb = sb("wg_sb", [P, E])
        bg_bc = sb("bg_bc", [P, E])
        b1_nat = sb("b1_nat", [E, 2 * P])
        b1c = sb("b1c", [P, 3, E])
        b2_sb = sb("b2_sb", [2 * E, D])
        w1_raw = sb("w1_raw", [P, 4, 2 * P])
        xn = sb("xn", [P, GB, D])
        xnt = sb("xnt", [P, GT])
        ctx_in = sb("ctx_in", [M, GB, D])
        ctx_t = sb("ctx_t", [P, GB, M])
        v0 = sb("v0", [M, GB, H, HD + 1])
        hq = sb("hq", [P, HR, P], F32R)
        hk = sb("hk", [P, HR, M], F32R)
        qx = sb("qx", [P, 2, HR, P], F32R)
        kx = sb("kx", [P, 2, HR, M], F32R)
        nmax = sb("nmax", [P, HG, HR])
        nmax_hi = sb("nmax_hi", [P, HG, HR], F32R)
        nt = sb("nt", [P, HG, 32])
        ntt = sb("ntt", [P, P], F32R)
        wide = sb("wide", [P, HG, HR * P])
        prob = wide[0:M, :, :]
        rden = sb("rden", [P, H])
        on = sb("on", [P, H, HD])
        ont = sb("ont", [P, P])
        xh = sb("xh", [P, GT], F32R)
        xl = sb("xl", [P, GT], F32R)
        lg = sb("lg", [P, GB, E])
        top = sb("top", [P, GB, 8])
        gw = sb("gw", [P, 6, GB, E])
        gs = sb("gs", [P, 4, GB])
        ghl = sb("ghl", [P, GB, 2 * E])
        ghr = sb("ghr", [P, GB, E], F32R)
        gt = sb("gt", [2 * E, GT], F32R)
        ea = rings[:, 0, :, :]
        ea7 = rings[:, 1, :, :]
        esg = rings[:, 2, :, :]
        eb = rings[:, 3, :, :]
        ec = rings[:, 4, :, :]
        eq = rings[:, 5, :, :]
        es = rings[:, 6, :, :]
        ys = sb("ys", [P, GT])
        qt = rings[:, 3, 0, :]
        mx1 = sb("mx1", [P, GB])
        sm1 = sb("sm1", [P, GB])
        rs1 = sb("rs1", [P, 2, GB])
        p1 = rings[:, 4, 0, 0:GB * M].rearrange("p (b m) -> p b m", b=GB)
        p1t = rings[0:M, 5, 0, :]
        bw = sb("bw", [P, 2, 2 * HID])
        bfly = sb("bfly", [P, 2, HID])
        bft = sb("bft", [P, HID])
        bbias = sb("bbias", [1, 2, HID])
        bbt = sb("bbt", [1, HID])
        wcon = sb("wcon", [P, HC, D])
        wup = sb("wup", [P, HID])
        wdn = sb("wdn", [P, HC, D])
        ubias = sb("ubias", [1, HID])
        upb = sb("upb", [P, HC])
        gh = wide[:, :, :]
        bcd = sb("bcd", [P, D])

        bank = [ctx.enter_context(nc.psum_tensor(f"bank{i}", [P, 512], F32)) for i in range(8)]
        SB, PK, PQ, TP, PO = bank[0:4], bank[4], bank[5], bank[6], bank[7]

        names = """ld_x ld_w ld_small ld_w1 ld_w2 ld_moe ld_ffn consts pick_rdy masks bst_rdy bst_rows w_turned w_rdy
            tanh_rdy xr_rdy ln_var ln_sqrt ln_rdy xn_rdy xn_turned xnt_rdy ctx_ld ctx_turned ctx_rdy v0_mm v0_rdy
            v1_mm v1_rdy k1_mm k1_rdy k_mm kh_rdy kx_rdy q_mm qh_rdy qx_rdy s_mm max_rdy nt_rdy nt_turned ntt_rdy
            st_mm exp_rdy pv_mm on_rdy on_turned ont_rdy o_mm x1_rdy w1_split w1_split_act b1_turned b1_rdy
            m_xn m_turned m_xnt m_xh m_xl m_lg_mm m_lg m_exp m_ghl m_g_turned m_gt m_ha m_hb m_gb m_a m_sg m_eb m_eq
            m_ec m_s m_y m_ys m_ys_turned m_x2 c_xn c_turned c_xnt c_q c_qt c_s c_max c_exp c_p_turned c_pt c_pv c_x3
            d_xn d_turned d_xnt d_h d_g d_o d_x4 d_out dve_own act_own pool_own bw_ld0 bw_ld1 bw_used wc_turned wc_rdy
            bf_rdy wd_turned wd_rdy ub_rdy ub_turned upb_rdy bst_ld""".split()
        s = {n: sem(n) for n in names}

        def bc(name):
            v = a[name]
            return bass.AP(tensor=v.tensor, offset=v.offset, ap=[[0, P], [1, v.shape[0]]])

        block = ctx.enter_context(nc.Block())

        @block.sync
        def _(sp):
            for g in range(G):
                sp.dma_start(x_sb[:, g * GB:(g + 1) * GB, :],
                             a["x"][g * GB:(g + 1) * GB].rearrange("b n d -> n b d")).then_inc(s["ld_x"], 16)
            for i, n in enumerate(["L0_xattn_Wq", "L0_xattn_Wk", "L0_xattn_Wv", "L0_xattn_Wo",
                                   "L1_xattn_Wq", "L1_xattn_Wk", "L1_xattn_Wv"]):
                sp.dma_start(wnat[:, i, :], a[n]).then_inc(s["ld_w"], 16)
            sp.wait_ge(s["bst_rdy"], 3)
            for j, rows in enumerate((bq_rows, bk_rows)):
                for lo, src in enumerate((bst_hi, bst_lo)):
                    sp.dma_start(rows[lo * HR:(lo + 1) * HR, :].bitcast(F32),
                                 src[:, j, :].bitcast(F32).rearrange("o (r c) -> o r c", r=HR)).then_inc(s["bst_ld"], 16)

            def context(g):
                if g >= 1:
                    sp.wait_ge(s["ctx_turned"], g)
                sp.dma_start(ctx_in[:, :, :], a["ctx_1024"][g * GB:(g + 1) * GB].rearrange("b m d -> m b d")
                             ).then_inc(s["ctx_ld"], 16)

            def stage_weights(k):
                if k >= 2:
                    sp.wait_ge(s["bw_used"], k - 1)
                t, i = ("L1_ffn_up_weights", k) if k < STAGES else ("L1_ffn_down_weights", 2 * STAGES - 1 - k)
                v = a[t]
                sp.dma_start(bw[:, k % 2, :], bass.AP(tensor=v.tensor, offset=v.offset + i * 2 * HID,
                                                      ap=[[0, P], [1, 2 * HID]])).then_inc(s[f"bw_ld{k % 2}"], 16)

            for k in range(2 * STAGES):
                if k in (2, 3, 6, 10):
                    context((2, 3, 6, 10).index(k))
                stage_weights(k)

            with sp.Fori(0, G) as g:
                sp.wait_ge(s["d_x4"], g + 1)
                sp.dma_start(out[bass.ts(g, GB)].rearrange("b n d -> n b d"),
                             xr[:, bass.ts(g, GB), :]).then_inc(s["d_out"], 16)
            sp.wait_ge(s["d_out"], 16 * G)

        @block.gpsimd
        def _(pool):
            own = Own(pool, s["pool_own"])
            own.then_wait(pool.memset(ident[:, :], 0.0))
            own.then_wait(pool.memset(ones_raw[:, :, :], 0.0))
            own.then_wait(pool.memset(pick_e_raw[:, :, :], 0.0))
            own.then_wait(pool.memset(mrow[:, :, :], 0.0))
            own.then_wait(pool.affine_select(out=ident[:, :], in_=ident[:, :], compare_op=ALU.not_equal, fill=1.0,
                                        base=0, pattern=[[-1, P]], channel_multiplier=1))
            for part in range(2):
                for gg in range(HG):
                    sl = ones_raw[32 * gg:32 * gg + 32, :, :]
                    own.then_wait(pool.affine_select(out=sl, in_=sl, compare_op=ALU.not_equal, fill=1.0,
                                                base=-HR * part, pattern=[[-1, HR], [0, P]],
                                                channel_multiplier=1))
                sl = pick_e_raw[:, :, :]
                own.then_wait(pool.affine_select(out=sl, in_=sl, compare_op=ALU.not_equal, fill=1.0,
                                            base=-E * part, pattern=[[-1, E], [0, P]], channel_multiplier=1))
            m4 = mrow[:, :, :].rearrange("o t (g c) -> o t g c", g=HG)
            own.then_wait(pool.memset(m4[:, 0, :, 2 * HD:3 * HD], -1.0))
            own.then_wait(pool.memset(m4[:, 1, :, HD:2 * HD], -1.0))
            own.then_wait(pool.memset(bst[:, :, :], 0.0))
            own.then_wait(pool.memset(wq_st[:, :, :, :], 0.0))
            own.then_wait(pool.memset(wk_st[:, :, :, :], 0.0))
            own.then_wait(pool.memset(nt[:, :, :], 0.0))
            pool.memset(v0[:, :, :, :], 1.0).then_inc(s["consts"], 1)
            pool.wait_ge(s["consts"], 1)

            pool.wait_ge(s["tanh_rdy"], 1)
            pool.wait_ge(s["ld_small"], 16 * 11)
            own.then_wait(pool.tensor_scalar(bcast[:, BO, :], bcast[:, BO, :], tg[:, 0:1], None, ALU.mult))
            pool.wait_ge(s["ld_x"], 16 * G)
            for b in range(NB):
                ins = pool.tensor_tensor(xr[:, b, :], x_sb[:, b, :], bcast[:, BO, :], ALU.add)
            ins.then_inc(s["xr_rdy"], 1)
            pool.wait_ge(s["xr_rdy"], 1)
            own.then_wait(pool.tensor_tensor(bcd[:, :], bcast[:, BC, :], bcast[:, BD, :], ALU.add))
            own.then_wait(pool.tensor_scalar(bcd[:, :], bcd[:, :], tg[:, 3:4], None, ALU.mult))

            def stage(w, st_i, src, tmp, dst, rows, transposed, signal=None):
                S = 2 ** st_i
                v = w[0:rows, :].rearrange("p (n s i j) -> p n i j s", s=S, i=2, j=2)
                if transposed:
                    v = w[0:rows, :].rearrange("p (n s j i) -> p n i j s", s=S, i=2, j=2)
                y = src.rearrange("p (n j s) -> p n j s", j=2, s=S)
                t = tmp.rearrange("p (n i s) -> p n i s", i=2, s=S)
                o = dst.rearrange("p (n i s) -> p n i s", i=2, s=S)
                for i in range(2):
                    own.mark(pool.tensor_tensor(t[:, :, i, :], v[:, :, i, 0, :], y[:, :, 0, :], ALU.mult))
                    own.mark(pool.tensor_tensor(o[:, :, i, :], v[:, :, i, 1, :], y[:, :, 1, :], ALU.mult))
                own.wait()
                ins = pool.tensor_tensor(dst, dst, tmp, ALU.add)
                if signal is None:
                    own.then_wait(ins)
                else:
                    ins.then_inc(s[signal[0]], 1)
                    pool.wait_ge(s[signal[0]], signal[1])

            pool.wait_ge(s["ld_ffn"], 16 * 4)
            for k in range(STAGES):
                pool.wait_ge(s[f"bw_ld{k % 2}"], 16 * (k // 2 + 1))
                w = bw[:, k % 2, :]
                last = k == STAGES - 1
                stage(w, k, bfly[:, k % 2, :], bft[:, :], wup[:, :] if last else bfly[:, (k + 1) % 2, :], P, False)
                stage(w, k, bbias[:, k % 2, :], bbt[:, :], bbias[:, (k + 1) % 2, :], 1, False,
                      ("bw_used", k + 1))
            pool.tensor_tensor(ubias[:, :], bbias[:, STAGES % 2, :], ubias[:, :], ALU.add).then_inc(s["ub_rdy"], 1)
            pool.wait_ge(s["ub_rdy"], 1)
            pool.wait_ge(s["wc_rdy"], 1)
            for k in range(STAGES):
                pool.wait_ge(s[f"bw_ld{(STAGES + k) % 2}"], 16 * ((STAGES + k) // 2 + 1))
                src = wdn[:, :, :].rearrange("p c d -> p (c d)") if k == 0 else bfly[:, k % 2, :]
                stage(bw[:, (STAGES + k) % 2, :], STAGES - 1 - k, src, bft[:, :],
                      bfly[:, (k + 1) % 2, :], P, True,
                      ("bw_used", STAGES + k + 1) if k < STAGES - 1 else ("bf_rdy", 1))

            for q in range(E // 4):
                pool.dma_start(w1_raw[:, :, :], a["L0_ffn_w1"][4 * q:4 * q + 4].rearrange("e h d -> h e d")
                               ).then_inc(s["ld_w1"], 16)
                pool.wait_ge(s["ld_w1"], 16 * (q + 1))
                src = w1_raw[:, :, :].rearrange("p e (i t) -> p e t i", t=2)
                for e in range(4):
                    own.mark(pool.tensor_copy(w1_hi[:, 4 * q + e, :, :], src[:, e, :, :]))
                own.wait()
                for e in range(4):
                    ins = pool.tensor_tensor(w1_lo[:, 4 * q + e, :, :], src[:, e, :, :],
                                             w1_hi[:, 4 * q + e, :, :].bitcast(F32), ALU.subtract)
                ins.then_inc(s["w1_split"], 1)
                pool.wait_ge(s["w1_split"], q + 1)

            with pool.Fori(0, G) as g:
                for e in range(E):
                    pool.wait_ge(s["m_ec"], g * E + e + 1)
                    pool.wait_ge(s["m_eq"], g * E + e + 1)
                    if e >= 2:
                        pool.wait_ge(s["m_y"], g * E + e - 1)
                    else:
                        pool.wait_ge(s["m_y"], g * E)
                    pool.tensor_tensor(es[:, e % 2, :], ec[:, e % 2, :], eq[:, e % 2, :],
                                       ALU.mult).then_inc(s["m_s"], 1)

        @block.scalar
        def _(act):
            own = Own(act, s["act_own"])
            for j, n in enumerate(("g_xattn", "g_ffn")):
                v = a[n]
                act.dma_start(graw[:, 2 * j:2 * j + 2], bc(n)).then_inc(s["ld_small"], 16)
            for j, n in enumerate(("L0_xattn_bv", "L0_xattn_bo", "L1_xattn_bv", "L1_ffn_b_con", "L1_ffn_down_bias")):
                act.dma_start(bcast[:, j, :], bc(n)).then_inc(s["ld_small"], 16)
            for j, n in enumerate(("L1_xattn_bq", "L1_xattn_bk")):
                act.dma_start(bcol[:, j:j + 1], a[n].rearrange("(p o) -> p o", o=1)).then_inc(s["ld_small"], 16)
            for j, n in enumerate(("L0_xattn_bq", "L0_xattn_bk")):
                act.dma_start(brow[:, j, :], a[n].rearrange("(o n) -> o n", o=1)).then_inc(s["ld_small"], 16)
            act.dma_start(bcol[:, 2:3], a["L0_ffn_norm_scale"].rearrange("(p o) -> p o", o=1)).then_inc(s["ld_moe"], 16)
            act.dma_start(wg_sb[:, :], a["L0_ffn_wg"]).then_inc(s["ld_moe"], 16)
            act.dma_start(bg_bc[:, :], bc("L0_ffn_bg")).then_inc(s["ld_moe"], 16)
            act.dma_start(b1_nat[:, :], a["L0_ffn_b1"]).then_inc(s["ld_moe"], 16)
            for j in range(2):
                act.dma_start(b2_sb[j * E:(j + 1) * E, :], a["L0_ffn_b2"]).then_inc(s["ld_moe"], 16)
            act.dma_start(bfly[:, 0, :], a["L1_ffn_W_exp"]).then_inc(s["ld_ffn"], 16)
            act.dma_start(bbias[:, 0, :], a["L1_ffn_b_exp"].rearrange("(o n) -> o n", o=1)).then_inc(s["ld_ffn"], 16)
            act.dma_start(ubias[:, :], a["L1_ffn_up_bias"].rearrange("(o n) -> o n", o=1)).then_inc(s["ld_ffn"], 16)
            act.dma_start(wcon[:, :, :], a["L1_ffn_W_con"].rearrange("(c p) d -> p c d", p=P)).then_inc(s["ld_ffn"], 16)

            act.wait_ge(s["ld_small"], 16 * 11)
            act.activation(tg[:, :], graw[:, :], ACT.Tanh).then_inc(s["tanh_rdy"], 1)

            def sqrt_var(n):
                act.wait_ge(s["ln_var"], n + 1)
                act.activation(st[:, 2, :], st[:, 1, :], ACT.Sqrt).then_inc(s["ln_sqrt"], 1)

            act.wait_ge(s["wc_turned"], 1)
            act.activation(wdn[:, :, :], PK[:, :].rearrange("p (c d) -> p c d", c=HC), ACT.Copy).then_inc(s["wc_rdy"], 1)
            sqrt_var(0)
            with act.Fori(0, G) as g:
                act.wait_ge(s["xn_turned"], g + 1)
                act.activation(xnt[:, :], TP[:, :], ACT.Copy).then_inc(s["xnt_rdy"], 1)
                act.wait_ge(s["ctx_turned"], g + 1)
                act.activation(ctx_t[:, :, :], PK[:, 0:GB * M].rearrange("p (b m) -> p b m", b=GB),
                               ACT.Copy).then_inc(s["ctx_rdy"], 1)
                act.wait_ge(s["k1_mm"], g + 1)
                act.activation(k1_all[:, bass.ts(g, GB * M)], PQ[:, 0:GB * M], ACT.Identity,
                               bias=bcol[:, 1:2]).then_inc(s["k1_rdy"], 1)

                def k_high(u):
                    act.wait_ge(s["k_mm"], g * GB + u + 1)
                    act.activation(hk[:, :, :], PK[:, 0:HR * M].rearrange("p (r m) -> p r m", r=HR),
                                   ACT.Copy).then_inc(s["kh_rdy"], 1)

                def q_high(u):
                    act.wait_ge(s["q_mm"], g * GB + u + 1)
                    act.activation(hq[:, :, :], PQ[:, :].rearrange("p (r m) -> p r m", r=HR),
                                   ACT.Copy).then_inc(s["qh_rdy"], 1)

                def neg_max_t(u):
                    act.wait_ge(s["nt_turned"], g * GB + u + 1)
                    act.activation(ntt[:, :], TP[:, 0:P], ACT.Copy).then_inc(s["ntt_rdy"], 1)

                def exps(u):
                    for gg in range(HG):
                        act.wait_ge(s["st_mm"], (g * GB + u) * HG + gg + 1)
                        act.activation(prob[:, gg, :], SB[gg][0:M, :], ACT.Exp,
                                       scale=SCALE).then_inc(s["exp_rdy"], 1)

                def attn_t(u):
                    act.wait_ge(s["on_turned"], g * GB + u + 1)
                    act.activation(ont[:, :], TP[:, 0:P], ACT.Copy).then_inc(s["ont_rdy"], 1)

                k_high(0)
                q_high(0)
                for u in range(-1, GB):
                    if u + 2 < GB:
                        k_high(u + 2)
                    if u + 1 < GB:
                        neg_max_t(u + 1)
                    if u + 2 < GB:
                        q_high(u + 2)
                    if u >= 0:
                        attn_t(u)
                    if u + 1 < GB:
                        exps(u + 1)

            act.wait_ge(s["xn_rdy"], G)
            act.wait_ge(s["xr_rdy"], 1)
            act.dma_start(w2_sb[:, :, :], a["L0_ffn_w2"].rearrange("e i h -> i e h")).then_inc(s["ld_w2"], 16)
            sqrt_var(1)
            sqrt_var(2)
            with act.Fori(0, G) as g:
                act.wait_ge(s["m_xnt"], g + 1)
                act.activation(xh[:, :], xnt[:, :], ACT.Copy).then_inc(s["m_xh"], 1)
                act.wait_ge(s["m_exp"], 2 * g + 1)
                act.activation(gw[:, 1, :, :], gw[:, 0, :, :], ACT.Exp).then_inc(s["m_exp"], 1)

                def expert(e):
                    act.wait_ge(s["m_ha"], g * E + e + 1)
                    act.wait_ge(s["m_ec"], g * E + max(e - 1, 0))
                    act.activation(ea[:, e % 2, :], SB[1 + e % 2][:, :], ACT.Identity,
                                   bias=b1c[:, 0, e:e + 1]).then_inc(s["m_a"], 1)
                    act.wait_ge(s["m_eq"], g * E + max(e - 1, 0))
                    act.activation(esg[:, e % 2, :], SB[1 + e % 2][:, :], ACT.Sigmoid, scale=ALPHA,
                                   bias=b1c[:, 2, e:e + 1]).then_inc(s["m_sg"], 1)

                expert(0)
                expert(1)
                act.wait_ge(s["m_g_turned"], g + 1)
                act.activation(gt[:, :], TP[0:2 * E, :], ACT.Copy).then_inc(s["m_gt"], 1)
                for e in range(2, E):
                    expert(e)
                act.wait_ge(s["m_y"], (g + 1) * E)
                act.activation(ys[:, :], SB[0][:, :], ACT.Copy).then_inc(s["m_ys"], 1)

            act.wait_ge(s["wd_turned"], 1)
            act.activation(wdn[:, :, :], PK[:, :].rearrange("p (c d) -> p c d", c=HC), ACT.Copy).then_inc(s["wd_rdy"], 1)
            sqrt_var(3)
            with act.Fori(0, G) as g:
                act.wait_ge(s["c_turned"], g + 1)
                act.activation(xnt[:, :], TP[:, :], ACT.Copy).then_inc(s["c_xnt"], 1)
                act.wait_ge(s["c_q"], g + 1)
                act.activation(qt[:, :], SB[0][:, :], ACT.Identity, bias=bcol[:, 0:1]).then_inc(s["c_qt"], 1)
                act.wait_ge(s["c_max"], g + 1)
                for u in range(GB):
                    act.activation(p1[:, u, :], SB[1][:, u * M:(u + 1) * M], ACT.Exp, bias=mx1[:, u:u + 1],
                                   accum_out=sm1[:, u:u + 1]).then_inc(s["c_exp"], 1)
                act.wait_ge(s["c_p_turned"], g + 1)
                act.activation(p1t[:, :], SB[2][0:M, :], ACT.Copy).then_inc(s["c_pt"], 1)
            sqrt_var(4)
            act.wait_ge(s["ub_turned"], 1)
            act.activation(upb[:, :], PQ[:, 0:HC], ACT.Copy).then_inc(s["upb_rdy"], 1)
            act.wait_ge(s["upb_rdy"], 1)
            with act.Fori(0, G) as g:
                act.wait_ge(s["d_turned"], g + 1)
                act.activation(xnt[:, :], TP[:, :], ACT.Copy).then_inc(s["d_xnt"], 1)
                for c in range(HC):
                    act.wait_ge(s["d_h"], g * HC + c + 1)
                    act.activation(gh[:, c, :], SB[c][:, :], ACT.Gelu, bias=upb[:, c:c + 1]).then_inc(s["d_g"], 1)

        @block.tensor
        def _(pe):
            pe.wait_ge(s["consts"], 1)
            pe.wait_ge(s["ld_w"], 16 * NW)
            for i in range(NW):
                mm = pe.transpose((SB[0] if i < 4 else SB[1])[:, (i % 4) * P:(i % 4 + 1) * P], wnat[:, i, :],
                                  ident[:, :])
            mm.then_inc(s["w_turned"], 1)
            for j in range(2):
                mm = pe.matmul(SB[2][:, j:j + 1], mrow[:, j, :], ident[0:1, 0:1], start=True, stop=True)
            mm.then_inc(s["w_turned"], 1)
            pe.wait_ge(s["ld_moe"], 16 * 6)
            for j in range(2):
                mm = pe.transpose(SB[3][:, j * E:(j + 1) * E], b1_nat[:, j:2 * P:2], ident[0:E, 0:E])
            mm.then_inc(s["b1_turned"], 1)
            pe.wait_ge(s["ld_ffn"], 16 * 4)
            for c in range(HC):
                mm = pe.transpose(PK[:, c * P:(c + 1) * P], wcon[:, c, :], ident[:, :])
            mm.then_inc(s["wc_turned"], 1)
            pe.wait_ge(s["w_rdy"], 1)
            pe.wait_ge(s["b1_rdy"], 1)
            pe.wait_ge(s["wc_rdy"], 1)
            pe.wait_ge(s["pick_rdy"], 1)
            pe.wait_ge(s["bst_ld"], 16 * 4)

            with pe.Fori(0, G) as g:
                pe.wait_ge(s["xn_rdy"], g + 1)
                pe.wait_ge(s["ont_rdy"], g * GB)
                for u in range(GB):
                    mm = pe.transpose(TP[:, u * P:(u + 1) * P], xn[:, u, :], ident[:, :])
                mm.then_inc(s["xn_turned"], 1)
                pe.wait_ge(s["ctx_ld"], 16 * g + 16)
                pe.wait_ge(s["kx_rdy"], g * GB)
                for u in range(GB):
                    mm = pe.transpose(PK[:, u * M:(u + 1) * M], ctx_in[:, u, :], ident[0:M, 0:M])
                mm.then_inc(s["ctx_turned"], 1)
                pe.wait_ge(s["ctx_rdy"], g + 1)
                pe.wait_ge(s["x1_rdy"], g * GB)
                for u in range(GB):
                    mm = pe.matmul(PO[0:M, u * P:(u + 1) * P], ctx_t[:, u, :], wt[:, WV0, :], start=True, stop=True)
                mm.then_inc(s["v0_mm"], 1)
                pe.wait_ge(s["qx_rdy"], g * GB)
                pe.matmul(PQ[:, 0:GB * M], wt[:, WK1, :], ctx_t[:, :, :], start=True, stop=True).then_inc(s["k1_mm"], 1)
                pe.wait_ge(s["xnt_rdy"], g + 1)
                for u in range(GB):
                    mm = pe.matmul(TP[0:M, u * P:(u + 1) * P], ctx_t[:, u, :], wt[:, WV1, :], start=True, stop=True)
                mm.then_inc(s["v1_mm"], 1)

                def k_stack(u):
                    if u >= 1:
                        pe.wait_ge(s["kx_rdy"], g * GB + u)
                    for r in range(HR):
                        o = PK[:, r * M:(r + 1) * M]
                        pe.matmul(o, bk_rows[:, :], pick[0:2 * HR, r, 0:M], start=True, stop=False)
                        mm = pe.matmul(o, wk_st[:, r, :, :], ctx_t[:, u, :], start=False, stop=True)
                    mm.then_inc(s["k_mm"], 1)

                def q_stack(u):
                    if u >= 1:
                        pe.wait_ge(s["qx_rdy"], g * GB + u)
                    else:
                        pe.wait_ge(s["k1_rdy"], g + 1)
                    for r in range(HR):
                        o = PQ[:, r * P:(r + 1) * P]
                        pe.matmul(o, bq_rows[:, :], pick[0:2 * HR, r, :], start=True, stop=False)
                        mm = pe.matmul(o, wq_st[:, r, :, :], xnt[:, u * P:(u + 1) * P], start=False, stop=True)
                    mm.then_inc(s["q_mm"], 1)

                def scores(u):
                    pe.wait_ge(s["kx_rdy"], g * GB + u + 1)
                    pe.wait_ge(s["qx_rdy"], g * GB + u + 1)
                    for gg in range(HG):
                        pe.wait_ge(s["exp_rdy"], (g * GB + u - 1) * HG + gg + 1 if u >= 1 else g * GB * HG)
                        p0 = 32 * gg
                        for r in range(HR):
                            mm = pe.matmul(SB[gg][:, r * M:(r + 1) * M], qx[p0:p0 + 32, u % 2, r, :],
                                           kx[p0:p0 + 32, u % 2, r, :], start=True, stop=True)
                        mm.then_inc(s["s_mm"], 1)

                def turn_max(u):
                    pe.wait_ge(s["nt_rdy"], g * GB + u + 1)
                    if u == 0:
                        pe.wait_ge(s["v1_rdy"], g + 1)
                    else:
                        pe.wait_ge(s["ont_rdy"], g * GB + u - 1)
                    pe.transpose(TP[:, 0:P], nt[:, :, :].rearrange("p g c -> p (g c)"), ident[:, :]).then_inc(s["nt_turned"], 1)

                def scores_t(u):
                    pe.wait_ge(s["ntt_rdy"], g * GB + u + 1)
                    for gg in range(HG):
                        pe.wait_ge(s["max_rdy"], (g * GB + u) * HG + gg + 1)
                        p0 = 32 * gg
                        for r in range(HR):
                            o = SB[gg][0:M, r * P:(r + 1) * P]
                            pe.matmul(o, kx[p0:p0 + 32, u % 2, r, :], qx[p0:p0 + 32, u % 2, r, :],
                                      start=True, stop=False)
                            mm = pe.matmul(o, pick[p0:p0 + 32, r, 0:M], ntt[p0:p0 + 32, :],
                                           start=False, stop=True)
                        mm.then_inc(s["st_mm"], 1)

                def values(u):
                    pe.wait_ge(s["exp_rdy"], (g * GB + u + 1) * HG)
                    if u == 0:
                        pe.wait_ge(s["v0_rdy"], g + 1)
                    else:
                        pe.wait_ge(s["x1_rdy"], g * GB + u)
                    for gg in range(HG):
                        for r in range(HR):
                            h = HG * r + gg
                            mm = pe.matmul(PO[:, h * (HD + 1):(h + 1) * (HD + 1)], prob[:, gg, r * P:(r + 1) * P],
                                           v0[:, u, h, :], start=True, stop=True)
                    mm.then_inc(s["pv_mm"], 1)

                def turn_attn(u):
                    pe.wait_ge(s["on_rdy"], g * GB + u + 1)
                    if u + 1 < GB:
                        pe.wait_ge(s["ntt_rdy"], g * GB + u + 2)
                    pe.transpose(TP[:, 0:P], on[:, :, :].rearrange("p h d -> p (h d)"), ident[:, :]).then_inc(s["on_turned"], 1)

                def project(u):
                    pe.wait_ge(s["ont_rdy"], g * GB + u + 1)
                    pe.matmul(PO[:, 256:256 + D], ont[:, :], wt[:, WO0, :], start=True, stop=True).then_inc(s["o_mm"], 1)

                k_stack(0)
                q_stack(0)
                for u in range(-1, GB):
                    if u + 1 < GB:
                        scores(u + 1)
                    if u >= 0:
                        values(u)
                    if u + 2 < GB:
                        k_stack(u + 2)
                    if u + 1 < GB:
                        turn_max(u + 1)
                    if u + 2 < GB:
                        q_stack(u + 2)
                    if u >= 0:
                        turn_attn(u)
                    if u + 1 < GB:
                        scores_t(u + 1)
                    if u >= 0:
                        project(u)

            pe.wait_ge(s["w1_split"], E // 4)
            pe.wait_ge(s["ld_w2"], 16)
            HA, HB_, GBK, Y = SB[1:3], (SB[3], PK), (PQ, PO), SB[0]
            pe.wait_ge(s["x1_rdy"], G * GB)
            with pe.Fori(0, G) as g:
                pe.wait_ge(s["m_xn"], g + 1)
                pe.wait_ge(s["m_x2"], g)
                for u in range(GB):
                    mm = pe.transpose(TP[:, u * P:(u + 1) * P], xn[:, u, :], ident[:, :])
                mm.then_inc(s["m_turned"], 1)
                pe.wait_ge(s["m_xnt"], g + 1)
                for u in range(GB):
                    mm = pe.matmul(TP[:, u * E:(u + 1) * E], xnt[:, u * P:(u + 1) * P], wg_sb[:, :],
                                   start=True, stop=True)
                mm.then_inc(s["m_lg_mm"], 1)
                pe.wait_ge(s["m_xh"], g + 1)
                pe.wait_ge(s["m_xl"], g + 1)

                def up(e):
                    pe.wait_ge(s["m_sg"], g * E + max(e - 1, 0))
                    pe.matmul(HA[e % 2][:, :], w1_hi[:, e, 0, :], xl[:, :], start=True, stop=False)
                    pe.matmul(HA[e % 2][:, :], w1_lo[:, e, 0, :], xh[:, :], start=False, stop=False)
                    pe.matmul(HA[e % 2][:, :], w1_hi[:, e, 0, :], xh[:, :], start=False, stop=True).then_inc(s["m_ha"], 1)
                    pe.wait_ge(s["m_eb"], g * E + max(e - 1, 0))
                    pe.matmul(HB_[e % 2][:, :], w1_hi[:, e, 1, :], xl[:, :], start=True, stop=False)
                    pe.matmul(HB_[e % 2][:, :], w1_lo[:, e, 1, :], xh[:, :], start=False, stop=False)
                    pe.matmul(HB_[e % 2][:, :], w1_hi[:, e, 1, :], xh[:, :], start=False, stop=True).then_inc(s["m_hb"], 1)

                def gate(e):
                    pe.wait_ge(s["m_eq"], g * E + max(e - 1, 0))
                    pe.matmul(GBK[e % 2][:, :], pick_e[:, e, :], gt[:, :], start=True, stop=True).then_inc(s["m_gb"], 1)

                def down(e):
                    pe.wait_ge(s["m_s"], g * E + e + 1)
                    pe.matmul(Y[:, :], w2_sb[:, e, :], es[:, e % 2, :], start=False, stop=(e == E - 1),
                              skip_group_check=True).then_inc(s["m_y"], 1)

                up(0)
                up(1)
                pe.wait_ge(s["m_ghl"], g + 1)
                for u in range(GB):
                    mm = pe.transpose(TP[0:2 * E, u * P:(u + 1) * P], ghl[:, u, :], ident[:, :])
                mm.then_inc(s["m_g_turned"], 1)
                pe.wait_ge(s["m_gt"], g + 1)
                pe.wait_ge(s["m_ys"], g)
                pe.matmul(Y[:, :], b2_sb[:, :], gt[:, :].bitcast(F32), start=True, stop=False, skip_group_check=True)
                gate(0)
                gate(1)
                for e in range(2, E):
                    up(e)
                    gate(e)
                    down(e - 2)
                down(E - 2)
                down(E - 1)
                pe.wait_ge(s["m_ys"], g + 1)
                for u in range(GB):
                    mm = pe.transpose(TP[:, u * P:(u + 1) * P], ys[:, u * P:(u + 1) * P], ident[:, :])
                mm.then_inc(s["m_ys_turned"], 1)

            pe.wait_ge(s["bf_rdy"], 1)
            for c in range(HC):
                mm = pe.transpose(PK[:, c * P:(c + 1) * P], bfly[:, STAGES % 2, c * P:(c + 1) * P], ident[:, :])
            mm.then_inc(s["wd_turned"], 1)
            pe.wait_ge(s["ub_rdy"], 1)
            pe.wait_ge(s["m_eq"], G * E)
            for c in range(HC):
                mm = pe.matmul(PQ[:, c:c + 1], ubias[:, c * P:(c + 1) * P], ident[0:1, 0:1], start=True, stop=True)
            mm.then_inc(s["ub_turned"], 1)

            with pe.Fori(0, G) as g:
                pe.wait_ge(s["c_xn"], g + 1)
                pe.wait_ge(s["c_xnt"], g)
                for u in range(GB):
                    mm = pe.transpose(TP[:, u * P:(u + 1) * P], xn[:, u, :], ident[:, :])
                mm.then_inc(s["c_turned"], 1)
                pe.wait_ge(s["c_xnt"], g + 1)
                pe.matmul(SB[0][:, :], wt[:, WQ1, :], xnt[:, :], start=True, stop=True).then_inc(s["c_q"], 1)
                pe.wait_ge(s["c_qt"], g + 1)
                for u in range(GB):
                    mm = pe.matmul(SB[1][:, u * M:(u + 1) * M], qt[:, u * P:(u + 1) * P],
                                   k1_all[:, bass.ds((g * GB + u) * M, M)], start=True, stop=True)
                mm.then_inc(s["c_s"], 1)
                pe.wait_ge(s["c_exp"], (g + 1) * GB)
                for u in range(GB):
                    mm = pe.transpose(SB[2][0:M, u * P:(u + 1) * P], p1[:, u, :], ident[:, :])
                mm.then_inc(s["c_p_turned"], 1)
                pe.wait_ge(s["c_pt"], g + 1)
                pe.wait_ge(s["c_x3"], g)
                for u in range(GB):
                    mm = pe.matmul(SB[3][:, u * P:(u + 1) * P], p1t[:, u * P:(u + 1) * P],
                                   v1_all[:, bass.ds(g * GB + u, 1), :], start=True, stop=True)
                mm.then_inc(s["c_pv"], 1)

            pe.wait_ge(s["wd_rdy"], 1)
            with pe.Fori(0, G) as g:
                pe.wait_ge(s["d_xn"], g + 1)
                pe.wait_ge(s["d_xnt"], g)
                for u in range(GB):
                    mm = pe.transpose(TP[:, u * P:(u + 1) * P], xn[:, u, :], ident[:, :])
                mm.then_inc(s["d_turned"], 1)
                pe.wait_ge(s["d_xnt"], g + 1)
                for c in range(HC):
                    pe.wait_ge(s["d_g"], g * HC)
                    pe.matmul(SB[c][:, :], wup[:, c * P:(c + 1) * P], xnt[:, :], start=True,
                              stop=True).then_inc(s["d_h"], 1)
                pe.wait_ge(s["d_g"], (g + 1) * HC)
                pe.wait_ge(s["d_x4"], g)
                for u in range(GB):
                    for c in range(HC):
                        mm = pe.matmul(PO[:, u * P:(u + 1) * P], gh[:, c, u * P:(u + 1) * P], wdn[:, c, :],
                                       start=(c == 0), stop=(c == HC - 1))
                mm.then_inc(s["d_o"], 1)

        @block.vector
        def _(dve):
            own = Own(dve, s["dve_own"])
            dve.wait_ge(s["consts"], 1)
            dve.tensor_copy(pick[:, :, :], ones_raw[:, :, :])
            dve.tensor_copy(pick_e[:, :, :], pick_e_raw[:, :, :]).then_inc(s["pick_rdy"], 1)
            dve.wait_ge(s["ld_small"], 16 * 11)
            for j in range(2):
                src = brow[:, j, :].rearrange("o (h d) -> o h d", d=HD)
                dst = bst[:, j, :].rearrange("o (h c) -> o h c", c=32)
                for c in range(C3):
                    own.mark(dve.tensor_copy(dst[:, :, c * HD:(c + 1) * HD], src))
            own.wait()
            dve.tensor_copy(bst_hi[:, :, :], bst[:, :, :]).then_inc(s["bst_rdy"], 1)
            dve.wait_ge(s["bst_rdy"], 1)
            dve.tensor_tensor(bst_lo[:, :, :], bst[:, :, :], bst_hi[:, :, :].bitcast(F32), ALU.subtract
                              ).then_inc(s["bst_rdy"], 1)
            dve.wait_ge(s["w_turned"], 2)
            dve.tensor_copy(nmask_q[:, :], SB[2][:, 0:1])
            dve.tensor_copy(nmask_k[:, :], SB[2][:, 1:2]).then_inc(s["bst_rdy"], 1)
            dve.tensor_copy(wt[:, 0:4, :], SB[0][:, :].rearrange("p (i c) -> p i c", i=4))
            dve.tensor_copy(wt[:, 4:NW, :], SB[1][:, 0:(NW - 4) * P].rearrange("p (i c) -> p i c", i=NW - 4))
            for i, dst in ((WQ0, wq_st), (WK0, wk_st)):
                src = SB[0][:, i * P:(i + 1) * P].rearrange("p (h d) -> p h d", d=HD)
                o = dst[:, :, :, :].rearrange("p r g c -> p (r g) c")
                for c in range(C3):
                    ins = dve.tensor_copy(o[:, :, c * HD:(c + 1) * HD], src)
            ins.then_inc(s["w_rdy"], 1)
            dve.wait_ge(s["b1_turned"], 1)
            own.mark(dve.tensor_copy(b1c[:, 0, :], SB[3][:, 0:E]))
            own.mark(dve.tensor_scalar(b1c[:, 1, :], SB[3][:, E:2 * E], 1.0, None, ALU.add))
            own.mark(dve.tensor_scalar(b1c[:, 2, :], SB[3][:, 0:E], ALPHA, None, ALU.mult))
            own.wait()
            dve.tensor_copy(st[:, 5, 0:1], b1c[:, 0, 0:1]).then_inc(s["b1_rdy"], 1)

            def rsqrt_steps(dst, n):
                dve.wait_ge(s["ln_sqrt"], n + 1)
                own.then_wait(dve.reciprocal(st[:, 3, :], st[:, 2, :]))
                own.then_wait(dve.tensor_tensor(st[:, 4, :], st[:, 3, :], st[:, 3, :], ALU.mult))
                own.then_wait(dve.tensor_tensor(st[:, 4, :], st[:, 4, :], st[:, 1, :], ALU.mult))
                own.then_wait(dve.tensor_scalar(st[:, 4, :], st[:, 4, :], -0.5, 1.5, ALU.mult, ALU.add))
                own.then_wait(dve.tensor_tensor(dst[:, :], st[:, 3, :], st[:, 4, :], ALU.mult))

            def layer_stats(n):
                own.mark(dve.tensor_tensor(mean[:, :], stats[:, :, 1], stats[:, :, 4], ALU.add))
                own.mark(dve.tensor_tensor(st[:, 0, :], stats[:, :, 1], stats[:, :, 4], ALU.subtract))
                own.mark(dve.tensor_tensor(st[:, 1, :], stats[:, :, 2], stats[:, :, 5], ALU.add))
                own.wait()
                own.mark(dve.tensor_scalar(mean[:, :], mean[:, :], 0.5, None, ALU.mult))
                own.mark(dve.tensor_tensor(st[:, 0, :], st[:, 0, :], st[:, 0, :], ALU.mult))
                own.mark(dve.tensor_scalar(st[:, 1, :], st[:, 1, :], 1.0 / D, EPS, ALU.mult, ALU.add))
                own.wait()
                dve.scalar_tensor_tensor(st[:, 1, :], st[:, 0, :], 0.25, st[:, 1, :], ALU.mult, ALU.add
                                         ).then_inc(s["ln_var"], 1)
                dve.wait_ge(s["ln_var"], n + 1)
                rsqrt_steps(rstd, n)

            def normed(g, sem_name):
                for u in range(GB):
                    b = bass.ds(g * GB + u, 1)
                    ins = dve.tensor_scalar(xn[:, u, :], xr[:, b, :].rearrange("p o d -> p (o d)"),
                                            mean[:, b], rstd[:, b], ALU.subtract, ALU.mult)
                ins.then_inc(s[sem_name], 1)

            dve.wait_ge(s["ld_x"], 16 * G)
            for b in range(NB):
                own.mark(dve.bn_stats(stats[:, b, :], x_sb[:, b, :]))
            own.wait()
            layer_stats(0)
            dve.wait_ge(s["xr_rdy"], 1)
            own.then_wait(dve.tensor_copy(st[:, 5, :], mean[:, :]))
            OWN_A, PER_A = own.base + own.n, 3 * GB
            with dve.Fori(0, G) as g:
                own.base, own.n = OWN_A + g * PER_A, 0
                for u in range(GB):
                    b = bass.ds(g * GB + u, 1)
                    ins = dve.tensor_scalar(xn[:, u, :], x_sb[:, b, :].rearrange("p o d -> p (o d)"),
                                            mean[:, b], rstd[:, b], ALU.subtract, ALU.mult)
                ins.then_inc(s["xn_rdy"], 1)
                dve.wait_ge(s["v0_mm"], g + 1)
                dve.tensor_tensor(v0[:, :, :, 0:HD],
                                  PO[0:M, :].rearrange("p (b h d) -> p b h d", b=GB, h=H),
                                  bcast[0:M, BV0, :].rearrange("p (h d) -> p h d", h=H).unsqueeze(1).to_broadcast([M, GB, H, HD]),
                                  ALU.add).then_inc(s["v0_rdy"], 1)
                dve.wait_ge(s["v1_mm"], g + 1)
                dve.tensor_tensor(v1_all[:, bass.ts(g, GB), :],
                                  TP[0:M, :].rearrange("p (b d) -> p b d", b=GB),
                                  bcast[0:M, BV1, :].unsqueeze(1).to_broadcast([M, GB, D]),
                                  ALU.add).then_inc(s["v1_rdy"], 1)

                def k_stacked(u):
                    dve.wait_ge(s["kh_rdy"], g * GB + u + 1)
                    dve.scalar_tensor_tensor(kx[:, u % 2, :, :], hk[:, :, :].bitcast(F32), nmask_k[:, 0:1],
                                             PK[:, 0:HR * M].rearrange("p (r m) -> p r m", r=HR),
                                             ALU.mult, ALU.add).then_inc(s["kx_rdy"], 1)

                def q_stacked(u):
                    dve.wait_ge(s["qh_rdy"], g * GB + u + 1)
                    dve.scalar_tensor_tensor(qx[:, u % 2, :, :], hq[:, :, :].bitcast(F32), nmask_q[:, 0:1],
                                             PQ[:, :].rearrange("p (r m) -> p r m", r=HR),
                                             ALU.mult, ALU.add).then_inc(s["qx_rdy"], 1)

                def maxima(u):
                    for gg in range(HG):
                        dve.wait_ge(s["s_mm"], (g * GB + u) * HG + gg + 1)
                        dve.tensor_reduce(nmax[:, gg, :], SB[gg][:, 0:HR * M].rearrange("p (r m) -> p r m", r=HR),
                                          AX.X, ALU.max, negate=True).then_inc(s["max_rdy"], 1)
                    dve.wait_ge(s["max_rdy"], (g * GB + u + 1) * HG)
                    own.then_wait(dve.tensor_copy(nmax_hi[:, :, :], nmax[:, :, :]))
                    dve.tensor_copy(nt[:, :, 0:HR], nmax_hi[:, :, :].bitcast(F32))
                    dve.tensor_tensor(nt[:, :, HR:2 * HR], nmax[:, :, :], nmax_hi[:, :, :].bitcast(F32),
                                      ALU.subtract).then_inc(s["nt_rdy"], 1)

                def weighted(u):
                    dve.wait_ge(s["pv_mm"], g * GB + u + 1)
                    pv = PO[:, 0:H * (HD + 1)].rearrange("p (h d) -> p h d", h=H)
                    own.then_wait(dve.reciprocal(rden[:, :], pv[:, :, HD]))
                    dve.tensor_tensor(on[:, :, :], pv[:, :, 0:HD], rden[:, :].unsqueeze(2).to_broadcast([P, H, HD]),
                                      ALU.mult).then_inc(s["on_rdy"], 1)

                def residual(u):
                    dve.wait_ge(s["o_mm"], g * GB + u + 1)
                    b = bass.ds(g * GB + u, 1)
                    row = xr[:, b, :].rearrange("p o d -> p (o d)")
                    dve.scalar_tensor_tensor(row, PO[:, 256:256 + D], tg[:, 0:1], row,
                                             ALU.mult, ALU.add).then_inc(s["x1_rdy"], 1)
                    dve.wait_ge(s["x1_rdy"], g * GB + u + 1)
                    own.mark(dve.bn_stats(stats[:, b, :].rearrange("p o s -> p (o s)"), row))

                k_stacked(0)
                q_stacked(0)
                for u in range(-1, GB):
                    if u + 1 < GB:
                        maxima(u + 1)
                    if u >= 0:
                        weighted(u)
                    if u + 2 < GB:
                        k_stacked(u + 2)
                        q_stacked(u + 2)
                    if u >= 0:
                        residual(u)
                assert own.n == PER_A
            own.base, own.n = OWN_A + G * PER_A, 0
            own.wait()
            layer_stats(1)

            own.then_wait(dve.tensor_tensor(st[:, 0, :], rstd[:, :], rstd[:, :], ALU.mult))
            own.then_wait(dve.tensor_scalar(st[:, 3, :], st[:, 1, :], -EPS, None, ALU.add))
            own.then_wait(dve.tensor_tensor(st[:, 0, :], st[:, 0, :], st[:, 3, :], ALU.mult))
            dve.tensor_scalar(st[:, 1, :], st[:, 0, :], EPS, None, ALU.add).then_inc(s["ln_var"], 1)
            dve.wait_ge(s["ln_var"], 3)
            rsqrt_steps(rms, 2)
            own.then_wait(dve.tensor_tensor(rms[:, :], rms[:, :], rstd[:, :], ALU.mult))
            OWN_B, PER_B = own.base + own.n, 33 + E
            with dve.Fori(0, G) as g:
                own.base, own.n = OWN_B + g * PER_B, 0
                for u in range(GB):
                    b = bass.ds(g * GB + u, 1)
                    ins = dve.tensor_scalar(xn[:, u, :], xr[:, b, :].rearrange("p o d -> p (o d)"),
                                            mean[:, b], rms[:, b], ALU.subtract, ALU.mult)
                ins.then_inc(s["m_xn"], 1)
                dve.wait_ge(s["m_turned"], g + 1)
                dve.tensor_scalar(xnt[:, :], TP[:, :], bcol[:, 2:3], None, ALU.mult).then_inc(s["m_xnt"], 1)
                dve.wait_ge(s["m_xh"], g + 1)
                dve.tensor_tensor(xl[:, :], xnt[:, :], xh[:, :].bitcast(F32), ALU.subtract).then_inc(s["m_xl"], 1)

                dve.wait_ge(s["m_lg_mm"], g + 1)
                own.then_wait(dve.tensor_tensor(lg[:, :, :], TP[:, 0:GB * E].rearrange("p (b e) -> p b e", b=GB),
                                                bg_bc[:, :].unsqueeze(1).to_broadcast([P, GB, E]), ALU.add))
                dve.tensor_copy(gs[:, 3, 0:1], lg[:, 0, 0:1])
                for u in range(GB):
                    own.mark(dve.max(top[:, u, :], lg[:, u, :]))
                own.wait()
                best = top[:, :, 0:1].to_broadcast([P, GB, E])
                fourth = top[:, :, 3:4].to_broadcast([P, GB, E])
                dve.tensor_tensor(gw[:, 0, :, :], lg[:, :, :], best, ALU.subtract).then_inc(s["m_exp"], 1)
                own.mark(dve.tensor_tensor(gw[:, 2, :, :], lg[:, :, :], fourth, ALU.is_gt))
                own.mark(dve.tensor_tensor(gw[:, 3, :, :], lg[:, :, :], fourth, ALU.is_equal))
                own.wait()
                own.mark(dve.tensor_reduce(gs[:, 0, :], gw[:, 2, :, :], AX.X, ALU.add))
                src = 3
                for k, step in enumerate((1, 2, 4, 8)):
                    dst = 4 + k % 2
                    own.mark(dve.tensor_copy(gw[:, dst, :, 0:step], gw[:, src, :, 0:step]))
                    own.mark(dve.tensor_tensor(gw[:, dst, :, step:E], gw[:, src, :, step:E],
                                               gw[:, src, :, 0:E - step], ALU.add))
                    own.wait()
                    src = dst
                own.then_wait(dve.tensor_tensor(gw[:, 4, :, :], gw[:, src, :, :],
                                                gs[:, 0, :].unsqueeze(2).to_broadcast([P, GB, E]), ALU.add))
                own.then_wait(dve.scalar_tensor_tensor(gw[:, 4, :, :], gw[:, 4, :, :], 4.5, gw[:, 3, :, :],
                                                       ALU.is_lt, ALU.mult))
                own.then_wait(dve.tensor_tensor(gw[:, 2, :, :], gw[:, 2, :, :], gw[:, 4, :, :], ALU.add))
                dve.wait_ge(s["m_exp"], 2 * g + 2)
                own.then_wait(dve.tensor_tensor(gw[:, 2, :, :], gw[:, 2, :, :], gw[:, 1, :, :], ALU.mult))
                own.then_wait(dve.tensor_reduce(gs[:, 1, :], gw[:, 2, :, :], AX.X, ALU.add))
                own.then_wait(dve.reciprocal(gs[:, 2, :], gs[:, 1, :]))
                own.then_wait(dve.tensor_tensor(gw[:, 2, :, :], gw[:, 2, :, :],
                                                gs[:, 2, :].unsqueeze(2).to_broadcast([P, GB, E]), ALU.mult))
                own.then_wait(dve.tensor_copy(ghr[:, :, :], gw[:, 2, :, :]))
                dve.tensor_copy(ghl[:, :, 0:E], ghr[:, :, :].bitcast(F32))
                dve.tensor_tensor(ghl[:, :, E:2 * E], gw[:, 2, :, :], ghr[:, :, :].bitcast(F32),
                                  ALU.subtract).then_inc(s["m_ghl"], 1)

                for e in range(E):
                    j = e % 2
                    dve.wait_ge(s["m_hb"], g * E + e + 1)
                    dve.tensor_scalar(eb[:, j, :], (SB[3], PK)[j][:, :], b1c[:, 1, e:e + 1], LIMIT + 1.0,
                                      ALU.add, ALU.min).then_inc(s["m_eb"], 1)
                    dve.wait_ge(s["m_a"], g * E + e + 1)
                    own.mark(dve.tensor_scalar(ea7[:, j, :], ea[:, j, :], LIMIT, None, ALU.min))
                    dve.wait_ge(s["m_s"], g * E + max(e - 1, 0))
                    own.wait()
                    dve.scalar_tensor_tensor(ec[:, j, :], eb[:, j, :], 1.0 - LIMIT, ea7[:, j, :],
                                             ALU.max, ALU.mult).then_inc(s["m_ec"], 1)
                    dve.wait_ge(s["m_sg"], g * E + e + 1)
                    dve.wait_ge(s["m_gb"], g * E + e + 1)
                    dve.scalar_tensor_tensor(eq[:, j, :], esg[:, j, :], SIG_LIMIT, (PQ, PO)[j][:, :],
                                             ALU.min, ALU.mult).then_inc(s["m_eq"], 1)
                for u in range(GB):
                    b = bass.ds(g * GB + u, 1)
                    own.mark(dve.tensor_scalar(xn[:, u, :], xr[:, b, :].rearrange("p o d -> p (o d)"),
                                               mean[:, b], rstd[:, b], ALU.subtract, ALU.mult))
                own.wait()
                dve.wait_ge(s["m_ys_turned"], g + 1)
                own.then_wait(dve.tensor_tensor(xn[:, :, :], xn[:, :, :],
                                                TP[:, :].rearrange("p (b d) -> p b d", b=GB), ALU.add))
                rows = xr[:, bass.ts(g, GB), :]
                dve.scalar_tensor_tensor(rows, xn[:, :, :], tg[:, 2:3], rows, ALU.mult, ALU.add
                                         ).then_inc(s["m_x2"], 1)
                dve.wait_ge(s["m_x2"], g + 1)
                for u in range(GB):
                    b = bass.ds(g * GB + u, 1)
                    own.mark(dve.bn_stats(stats[:, b, :].rearrange("p o s -> p (o s)"),
                                          xr[:, b, :].rearrange("p o d -> p (o d)")))
                assert own.n == PER_B, own.n
            own.base, own.n = OWN_B + G * PER_B, 0
            own.wait()
            layer_stats(3)

            OWN_C, PER_C = own.base + own.n, 2 + GB
            with dve.Fori(0, G) as g:
                own.base, own.n = OWN_C + g * PER_C, 0
                normed(g, "c_xn")
                dve.wait_ge(s["c_s"], g + 1)
                dve.tensor_reduce(mx1[:, :], SB[1][:, 0:GB * M].rearrange("p (b m) -> p b m", b=GB),
                                  AX.X, ALU.max, negate=True).then_inc(s["c_max"], 1)
                dve.wait_ge(s["c_exp"], (g + 1) * GB)
                own.then_wait(dve.reciprocal(rs1[:, 0, :], sm1[:, :]))
                own.then_wait(dve.tensor_scalar(rs1[:, 1, :], rs1[:, 0, :], tg[:, 1:2], None, ALU.mult))
                dve.wait_ge(s["c_pv"], g + 1)
                for u in range(GB):
                    row = xr[:, bass.ds(g * GB + u, 1), :].rearrange("p o d -> p (o d)")
                    ins = dve.scalar_tensor_tensor(row, SB[3][:, u * P:(u + 1) * P], rs1[:, 1, u:u + 1], row,
                                                   ALU.mult, ALU.add)
                ins.then_inc(s["c_x3"], 1)
                dve.wait_ge(s["c_x3"], g + 1)
                for u in range(GB):
                    b = bass.ds(g * GB + u, 1)
                    own.mark(dve.bn_stats(stats[:, b, :].rearrange("p o s -> p (o s)"),
                                          xr[:, b, :].rearrange("p o d -> p (o d)")))
                assert own.n == PER_C
            own.base, own.n = OWN_C + G * PER_C, 0
            own.wait()
            layer_stats(4)

            OWN_D = own.base + own.n
            with dve.Fori(0, G) as g:
                own.base, own.n = OWN_D + g, 0
                normed(g, "d_xn")
                rows = xr[:, bass.ts(g, GB), :]
                dve.wait_ge(s["d_turned"], g + 1)
                own.then_wait(dve.tensor_tensor(rows, rows, bcd[:, :].unsqueeze(1).to_broadcast([P, GB, D]), ALU.add))
                dve.wait_ge(s["d_o"], g + 1)
                dve.scalar_tensor_tensor(rows, PO[:, :].rearrange("p (b d) -> p b d", b=GB), tg[:, 3:4], rows,
                                         ALU.mult, ALU.add).then_inc(s["d_x4"], 1)


_INS = ["x", "ctx_1024", "g_xattn", "g_ffn", "L0_xattn_Wq", "L0_xattn_bq", "L0_xattn_Wk", "L0_xattn_bk",
        "L0_xattn_Wv", "L0_xattn_bv", "L0_xattn_Wo", "L0_xattn_bo", "L0_ffn_norm_scale", "L0_ffn_wg",
        "L0_ffn_bg", "L0_ffn_w1", "L0_ffn_b1", "L0_ffn_w2", "L0_ffn_b2", "L1_xattn_Wq", "L1_xattn_bq",
        "L1_xattn_Wk", "L1_xattn_bk", "L1_xattn_Wv", "L1_xattn_bv", "L1_ffn_W_exp", "L1_ffn_b_exp",
        "L1_ffn_up_weights", "L1_ffn_up_bias", "L1_ffn_down_weights", "L1_ffn_W_con", "L1_ffn_b_con",
        "L1_ffn_down_bias"]


def kernel(**inputs):
    import concourse.bacc as bacc
    from concourse.bass_utils import run_bass_kernel_spmd

    nc = bacc.Bacc("TRN2", target_bir_lowering=False, num_devices=1)
    arrays, aps = {}, {}
    for name in _INS:
        v = np.ascontiguousarray(inputs[name])
        arrays[f"in_{name}"] = v
        aps[name] = nc.dram_tensor(f"in_{name}", v.shape, mybir.dt.from_np(v.dtype), kind="ExternalInput").ap()
    shape = arrays["in_x"].shape
    out = nc.dram_tensor("out", shape, F32, kind="ExternalOutput").ap()
    flamingo_layers(nc, aps, out)
    r = run_bass_kernel_spmd(nc, [arrays], core_ids=[0])
    return r.results[0]["out"]
```

```python
from contextlib import ExitStack

import numpy as np

import concourse.bass as bass
from concourse import mybir

F32 = mybir.dt.float32
F32R = mybir.dt.float32r
ALU = mybir.AluOpType
ACT = mybir.ActivationFunctionType
AX = mybir.AxisListType

P = 128
GB = 4
LIMIT = 7.0
ALPHA = 1.702
EPS = 1e-5
SIG_LIMIT = float(1.0 / (1.0 + np.exp(-ALPHA * LIMIT)))


class Own:

    def __init__(self, eng, sem):
        self.eng, self.sem, self.n, self.base = eng, sem, 0, 0

    def then_wait(self, ins):
        ins.then_inc(self.sem, 1)
        self.n += 1
        self.eng.wait_ge(self.sem, self.base + self.n)

    def mark(self, ins):
        ins.then_inc(self.sem, 1)
        self.n += 1

    def wait(self):
        self.eng.wait_ge(self.sem, self.base + self.n)


def flamingo_layers(nc, a, out):
    NB, NT, D = a["x"].shape
    M = a["ctx_1024"].shape[1]
    E = a["L0_ffn_wg"].shape[1]
    HD = 8
    H = D // HD
    HG = 4
    HR = H // HG
    G = NB // GB
    GT = GB * NT
    HID = a["L1_ffn_W_exp"].shape[1]
    HC = HID // P
    STAGES = a["L1_ffn_up_weights"].shape[0]
    LAG, XT_AT, LG_AT, CX_AT, CQ_AT, CS_AT, EXP_AT, CP_AT, CV_AT, GT_AT = 3, 6, 7, 8, 9, 10, 11, 12, 13, 15
    SCALE = HD ** -0.5
    assert NT == P and D == P and H == HG * HR

    with ExitStack() as ctx:
        def sb(name, shape, dt=F32):
            return ctx.enter_context(nc.sbuf_tensor(name, shape, dt))

        def sem(name):
            return ctx.enter_context(nc.semaphore(name))

        x_sb = sb("x_sb", [P, NB, D])
        xr = sb("xr", [P, NB, D])
        v1_all = sb("v1_all", [M, NB, D])
        k1_all = sb("k1_all", [P, NB * M])
        w1_hi = sb("w1_hi", [P, E, 2, P], F32R)
        w1_lo = sb("w1_lo", [P, E, 2, P], F32R)
        w2_sb = x_sb
        stats = sb("stats", [P, NB, 6])
        mean = sb("mean", [P, NB])
        rstd = sb("rstd", [P, NB])
        rms = sb("rms", [P, NB])
        st = sb("st", [P, 6, NB])
        rings = sb("rings", [P, 7, 2, GT])
        ident = sb("ident", [P, P])
        pick_e_raw = rings[0:32, 0:2, :, :].rearrange("p a b (c m) -> p (a b c) m", m=P)
        pick_e = sb("pick_e", [32, E, P], F32R)
        NW = 7
        wnat = sb("wnat", [P, NW, P])
        wt = sb("wt", [P, NW, P])
        WQ0, WK0, WV0, WO0, WQ1, WK1, WV1 = range(NW)
        wq_st = sb("wq_st", [P, HR, HG, 32])
        wk_st = sb("wk_st", [P, HR, HG, 32])
        brow = sb("brow", [1, 2, P])
        bst = rings[0:1, 3, :, :]
        bst_c = sb("bst_c", [P, 2, HR])
        bcast = sb("bcast", [P, 5, D])
        BV0, BO, BV1, BC, BD = range(5)
        bcol = sb("bcol", [P, 3])
        tg = sb("tg", [P, 4])
        graw = sb("graw", [P, 4])
        wg_sb = sb("wg_sb", [P, E])
        bg_bc = sb("bg_bc", [P, E])
        b1_nat = sb("b1_nat", [E, 2 * P])
        b1c = sb("b1c", [P, 3, E])
        b2_sb = sb("b2_sb", [2 * E, D])
        xhl = sb("xhl", [P, 2, 2 * GT], F32R)
        xn = sb("xn", [P, GB, D])
        xnt = sb("xnt", [P, GT])
        ctx_in = sb("ctx_in", [M, GB, D])
        ctx_t = sb("ctx_t", [P, GB, M])
        vst = sb("vst", [M, GB, H, 32])
        qs = sb("qs", [P, 2, HR, P])
        ks = sb("ks", [P, 2, HR, M])
        nt = sb("nt", [P, HG, 32])
        ot = sb("ot", [P, 2 * P])
        wide = sb("wide", [P, HG, HR * P])
        prob = wide[0:M, :, :]
        rden = sb("rden", [P, H])
        on = sb("on", [P, H, HD])
        ont = sb("ont", [P, P])
        lg = sb("lg", [P, GB, E])
        top = sb("top", [P, GB, 8])
        gw = sb("gw", [P, 6, GB, E])
        gs = sb("gs", [P, 4, GB])
        ghl = sb("ghl", [P, GB, 2 * E])
        ghr = sb("ghr", [P, GB, E], F32R)
        gt = sb("gt", [2 * E, GT], F32R)
        ea = rings[:, 0, :, :]
        esg = rings[:, 1, :, :]
        eb = rings[:, 3, :, :]
        ec = rings[:, 4, :, :]
        eq = rings[:, 5, :, :]
        es = (rings[:, 6, 0, :], rings[:, 6, 1, :], wide[:, 2, :], wide[:, 3, :])
        ys = wide[:, 0, :]
        xo = wide[:, 1, :].rearrange("p (b d) -> p b d", b=GB)
        xc = xo
        xct = rings[:, 2, 0, :]
        qt = rings[:, 2, 1, :]
        mx1 = sb("mx1", [P, GB])
        sm1 = sb("sm1", [P, GB])
        rs1 = sb("rs1", [P, 2, GB])
        p1 = qs[:, 0, :, 0:M]
        p1t = ctx_in[:, :, :].rearrange("m b d -> m (b d)")
        cst = sb("cst", [P, GB, 6])
        cmean = sb("cmean", [P, GB])
        crstd = sb("crstd", [P, GB])
        cs = sb("cs", [P, 5, NB])
        minus_half = sb("minus_half", [P, 1])
        bw = sb("bw", [P, 2, 2 * HID])
        w1_raw = bw[:, 0, :].rearrange("p (e c) -> p e c", e=4)
        bfly = sb("bfly", [P, 2, HID])
        bft = sb("bft", [P, HID])
        bbias = sb("bbias", [1, 2, HID])
        bbt = sb("bbt", [1, HID])
        wcon = sb("wcon", [P, HC, D])
        wup = sb("wup", [P, HID])
        wdn = sb("wdn", [P, HC, D])
        ubias = sb("ubias", [1, HID])
        upb = sb("upb", [P, HC])
        gh = x_sb[:, :, :].rearrange("p (c b) d -> p c (b d)", c=HC)
        bcd = sb("bcd", [P, D])

        bank = [ctx.enter_context(nc.psum_tensor(f"bank{i}", [P, 512], F32)) for i in range(8)]
        SB, PK, PQ, TP, PO = bank[0:4], bank[4], bank[5], bank[6], bank[7]

        names = """ld_x ld_w ld_small ld_w1 ld_w2 ld_moe ld_ffn consts pick_rdy bst_rdy bst_turned bst_c_rdy w_turned w_rdy
            tanh_rdy xr_rdy ln_var ln_sqrt ln_rdy xn_rdy xn_turned xnt_rdy ctx_ld ctx_turned ctx_rdy v0_mm v0_rdy
            v1_mm v1_rdy k1_mm k1_rdy k_mm kx_rdy q_mm qx_rdy s_mm max_rdy nt_rdy nt_turned
            st_mm exp_rdy pv_mm on_rdy on_turned ont_rdy o_mm x1_rdy w1_split w1_split_act b1_turned b1_rdy
            m_xn m_turned m_xnt m_xh m_xl m_lg_mm m_lgd m_exp m_ghl m_g_turned m_gt m_ha m_hb m_gb m_a m_sg m_eb m_eq
            m_ec m_s m_y m_ys m_ys_turned m_x2 c_xn c_turned c_xnt c_q c_qt c_s c_max c_exp c_p_turned c_pt c_pv c_x3
            ln2_var ln2_pow d_xn d_turned d_xnt d_h d_g d_o d_x4 d_out dve_own act_own pool_own bw_ld0 bw_ld1 bw_used wc_turned wc_rdy
            bf_rdy wd_turned wd_rdy ub_rdy ub_turned upb_rdy ot_rdy ot_turned ntq_rdy""".split()
        s = {n: sem(n) for n in names}

        def bc(name):
            v = a[name]
            return bass.AP(tensor=v.tensor, offset=v.offset, ap=[[0, P], [1, v.shape[0]]])

        def need(eng, name, value):
            if not isinstance(value, int) or value > 0:
                eng.wait_ge(s[name], value)

        def pipelined(eng, body):
            body(0)
            with eng.Fori(1, G - 1) as g:
                body(g)
            body(G - 1)

        def first(g):
            return isinstance(g, int) and g == 0

        def last(g):
            return isinstance(g, int) and g == G - 1

        def high(g):
            return xhl[:, :, :].rearrange("p s c -> p (s c)")[:, bass.ds((g % 2) * 2 * GT, GT)]

        def low(g):
            return xhl[:, :, :].rearrange("p s c -> p (s c)")[:, bass.ds((g % 2) * 2 * GT + GT, GT)]

        def steps(eng, body):
            body(0)
            with eng.Fori(1, G) as g:
                body(g)

        block = ctx.enter_context(nc.Block())

        @block.sync
        def _(sp):
            for g in range(G):
                sp.dma_start(x_sb[:, g * GB:(g + 1) * GB, :],
                             a["x"][g * GB:(g + 1) * GB].rearrange("b n d -> n b d")).then_inc(s["ld_x"], 16)
            for i, n in enumerate(["L0_xattn_Wq", "L0_xattn_Wk", "L0_xattn_Wv", "L0_xattn_Wo",
                                   "L1_xattn_Wq", "L1_xattn_Wk", "L1_xattn_Wv"]):
                sp.dma_start(wnat[:, i, :], a[n]).then_inc(s["ld_w"], 16)
            def context(g):
                if g >= 1:
                    sp.wait_ge(s["ctx_turned"], g)
                sp.dma_start(ctx_in[:, :, :], a["ctx_1024"][g * GB:(g + 1) * GB].rearrange("b m d -> m b d")
                             ).then_inc(s["ctx_ld"], 16)

            def stage_weights(k):
                if k >= 2:
                    sp.wait_ge(s["bw_used"], k - 1)
                t, i = ("L1_ffn_up_weights", k) if k < STAGES else ("L1_ffn_down_weights", 2 * STAGES - 1 - k)
                v = a[t]
                sp.dma_start(bw[:, k % 2, :], bass.AP(tensor=v.tensor, offset=v.offset + i * 2 * HID,
                                                      ap=[[0, P], [1, 2 * HID]])).then_inc(s[f"bw_ld{k % 2}"], 16)

            for k in range(2 * STAGES):
                if k in (2, 3, 6, 10):
                    context((2, 3, 6, 10).index(k))
                stage_weights(k)

            for g in range(G):
                sp.wait_ge(s["d_x4"], g + 1)
                sp.dma_start(out[g * GB:(g + 1) * GB].rearrange("b n d -> n b d"),
                             xr[:, g * GB:(g + 1) * GB, :]).then_inc(s["d_out"], 16)
            sp.wait_ge(s["d_out"], 16 * G)

        @block.gpsimd
        def _(pool):
            own = Own(pool, s["pool_own"])
            own.then_wait(pool.memset(ident[:, :], 0.0))
            own.then_wait(pool.memset(pick_e_raw[:, :, :], 0.0))
            own.then_wait(pool.affine_select(out=ident[:, :], in_=ident[:, :], compare_op=ALU.not_equal, fill=1.0,
                                        base=0, pattern=[[-1, P]], channel_multiplier=1))
            for part in range(2):
                sl = pick_e_raw[:, :, :]
                own.then_wait(pool.affine_select(out=sl, in_=sl, compare_op=ALU.not_equal, fill=1.0,
                                                 base=-E * part, pattern=[[-1, E], [0, P]], channel_multiplier=1))
            own.then_wait(pool.memset(bst[:, :, :], 0.0))
            for r in range(HR):
                own.then_wait(pool.memset(bst[:, 1, r * P + HD + r:(r + 1) * P:32], 1.0))
            own.then_wait(pool.memset(wq_st[:, :, :, :], 0.0))
            own.then_wait(pool.memset(wk_st[:, :, :, :], 0.0))
            own.then_wait(pool.memset(nt[:, :, :], 0.0))
            own.then_wait(pool.memset(minus_half[:, :], -0.5))
            own.then_wait(pool.memset(vst[:, :, :, :], 0.0))
            pairs = vst[:, :, :, :].rearrange("p b (x i) c -> p b x i c", i=2)
            own.then_wait(pool.memset(pairs[:, :, :, 0, HD:HD + 1], 1.0))
            pool.memset(pairs[:, :, :, 1, 16 + HD:16 + HD + 1], 1.0).then_inc(s["consts"], 1)
            pool.wait_ge(s["consts"], 1)

            pool.wait_ge(s["tanh_rdy"], 1)
            pool.wait_ge(s["ld_small"], 16 * 11)
            own.then_wait(pool.tensor_scalar(bcast[:, BO, :], bcast[:, BO, :], tg[:, 0:1], None, ALU.mult))
            pool.wait_ge(s["ld_x"], 16 * G)
            for b in range(NB):
                ins = pool.tensor_tensor(xr[:, b, :], x_sb[:, b, :], bcast[:, BO, :], ALU.add)
            ins.then_inc(s["xr_rdy"], 1)
            pool.wait_ge(s["xr_rdy"], 1)
            own.then_wait(pool.tensor_tensor(bcd[:, :], bcast[:, BC, :], bcast[:, BD, :], ALU.add))
            own.then_wait(pool.tensor_scalar(bcd[:, :], bcd[:, :], tg[:, 3:4], None, ALU.mult))

            def stage(w, st_i, src, tmp, dst, rows, transposed, signal=None):
                S = 2 ** st_i
                v = w[0:rows, :].rearrange("p (n s i j) -> p n i j s", s=S, i=2, j=2)
                if transposed:
                    v = w[0:rows, :].rearrange("p (n s j i) -> p n i j s", s=S, i=2, j=2)
                y = src.rearrange("p (n j s) -> p n j s", j=2, s=S)
                t = tmp.rearrange("p (n i s) -> p n i s", i=2, s=S)
                o = dst.rearrange("p (n i s) -> p n i s", i=2, s=S)
                for i in range(2):
                    own.mark(pool.tensor_tensor(t[:, :, i, :], v[:, :, i, 0, :], y[:, :, 0, :], ALU.mult))
                    own.mark(pool.tensor_tensor(o[:, :, i, :], v[:, :, i, 1, :], y[:, :, 1, :], ALU.mult))
                own.wait()
                ins = pool.tensor_tensor(dst, dst, tmp, ALU.add)
                if signal is None:
                    own.then_wait(ins)
                else:
                    ins.then_inc(s[signal[0]], 1)
                    pool.wait_ge(s[signal[0]], signal[1])

            pool.wait_ge(s["ld_ffn"], 16 * 4)
            for k in range(STAGES):
                pool.wait_ge(s[f"bw_ld{k % 2}"], 16 * (k // 2 + 1))
                w = bw[:, k % 2, :]
                top_stage = k == STAGES - 1
                stage(w, k, bfly[:, k % 2, :], bft[:, :], wup[:, :] if top_stage else bfly[:, (k + 1) % 2, :], P, False)
                stage(w, k, bbias[:, k % 2, :], bbt[:, :], bbias[:, (k + 1) % 2, :], 1, False,
                      ("bw_used", k + 1))
            pool.tensor_tensor(ubias[:, :], bbias[:, STAGES % 2, :], ubias[:, :], ALU.add).then_inc(s["ub_rdy"], 1)
            pool.wait_ge(s["ub_rdy"], 1)
            pool.wait_ge(s["wc_rdy"], 1)
            for k in range(STAGES):
                pool.wait_ge(s[f"bw_ld{(STAGES + k) % 2}"], 16 * ((STAGES + k) // 2 + 1))
                src = wdn[:, :, :].rearrange("p c d -> p (c d)") if k == 0 else bfly[:, k % 2, :]
                stage(bw[:, (STAGES + k) % 2, :], STAGES - 1 - k, src, bft[:, :],
                      bfly[:, (k + 1) % 2, :], P, True,
                      ("bw_used", STAGES + k + 1) if k < STAGES - 1 else ("bf_rdy", 1))

            for q in range(E // 4):
                pool.dma_start(w1_raw, a["L0_ffn_w1"][4 * q:4 * q + 4].rearrange("e h d -> h e d")
                               ).then_inc(s["ld_w1"], 16)
                pool.wait_ge(s["ld_w1"], 16 * (q + 1))
                src = w1_raw.rearrange("p e (i t) -> p e t i", t=2)
                for e in range(4):
                    own.mark(pool.tensor_copy(w1_hi[:, 4 * q + e, :, :], src[:, e, :, :]))
                own.wait()
                for e in range(4):
                    ins = pool.tensor_tensor(w1_lo[:, 4 * q + e, :, :], src[:, e, :, :],
                                             w1_hi[:, 4 * q + e, :, :].bitcast(F32), ALU.subtract)
                ins.then_inc(s["w1_split"], 1)
                pool.wait_ge(s["w1_split"], q + 1)

            def remainders(g):
                pool.wait_ge(s["m_xh"], g + 1)
                pool.tensor_tensor(low(g), xnt[:, :], high(g).bitcast(F32), ALU.subtract).then_inc(s["m_xl"], 1)

            def product(g, e):
                n = g * E + e + 1
                pool.wait_ge(s["m_ec"], n)
                need(pool, "m_y", n - len(es))
                pool.tensor_tensor(es[e % len(es)], ea[:, e % 2, :], ec[:, e % 2, :], ALU.mult).then_inc(s["m_s"], 1)

            def inverse_root(k, n):
                pool.wait_ge(s["ln2_var"], k)
                pool.tensor_tensor(cs[:, 1, 0:n], cs[:, 0, 0:n], minus_half[:, 0:1].to_broadcast([P, n]), ALU.pow
                                   ).then_inc(s["ln2_pow"], 1)

            def mixture(g):
                for e in range(E):
                    product(g, e)
                    if e == LAG + 2 and not first(g):
                        inverse_root(g, GB)
                    if e == XT_AT and not last(g):
                        remainders(g + 1)

            remainders(0)
            pipelined(pool, mixture)
            inverse_root(G, 3 * GB)
            inverse_root(G + 1, GB)
            inverse_root(G + 2, GB)

        @block.scalar
        def _(act):
            own = Own(act, s["act_own"])
            for j, n in enumerate(("g_xattn", "g_ffn")):
                v = a[n]
                act.dma_start(graw[:, 2 * j:2 * j + 2], bc(n)).then_inc(s["ld_small"], 16)
            for j, n in enumerate(("L0_xattn_bv", "L0_xattn_bo", "L1_xattn_bv", "L1_ffn_b_con", "L1_ffn_down_bias")):
                act.dma_start(bcast[:, j, :], bc(n)).then_inc(s["ld_small"], 16)
            for j, n in enumerate(("L1_xattn_bq", "L1_xattn_bk")):
                act.dma_start(bcol[:, j:j + 1], a[n].rearrange("(p o) -> p o", o=1)).then_inc(s["ld_small"], 16)
            for j, n in enumerate(("L0_xattn_bq", "L0_xattn_bk")):
                act.dma_start(brow[:, j, :], a[n].rearrange("(o n) -> o n", o=1)).then_inc(s["ld_small"], 16)
            act.dma_start(bcol[:, 2:3], a["L0_ffn_norm_scale"].rearrange("(p o) -> p o", o=1)).then_inc(s["ld_moe"], 16)
            act.dma_start(wg_sb[:, :], a["L0_ffn_wg"]).then_inc(s["ld_moe"], 16)
            act.dma_start(bg_bc[:, :], bc("L0_ffn_bg")).then_inc(s["ld_moe"], 16)
            act.dma_start(b1_nat[:, :], a["L0_ffn_b1"]).then_inc(s["ld_moe"], 16)
            for j in range(2):
                act.dma_start(b2_sb[j * E:(j + 1) * E, :], a["L0_ffn_b2"]).then_inc(s["ld_moe"], 16)
            act.dma_start(bfly[:, 0, :], a["L1_ffn_W_exp"]).then_inc(s["ld_ffn"], 16)
            act.dma_start(bbias[:, 0, :], a["L1_ffn_b_exp"].rearrange("(o n) -> o n", o=1)).then_inc(s["ld_ffn"], 16)
            act.dma_start(ubias[:, :], a["L1_ffn_up_bias"].rearrange("(o n) -> o n", o=1)).then_inc(s["ld_ffn"], 16)
            act.dma_start(wcon[:, :, :], a["L1_ffn_W_con"].rearrange("(c p) d -> p c d", p=P)).then_inc(s["ld_ffn"], 16)

            act.wait_ge(s["ld_small"], 16 * 11)
            act.activation(tg[:, :], graw[:, :], ACT.Tanh).then_inc(s["tanh_rdy"], 1)

            def sqrt_var(n):
                act.wait_ge(s["ln_var"], n + 1)
                act.activation(st[:, 2, :], st[:, 1, :], ACT.Sqrt).then_inc(s["ln_sqrt"], 1)

            act.wait_ge(s["wc_turned"], 1)
            act.activation(wdn[:, :, :], PK[:, :].rearrange("p (c d) -> p c d", c=HC), ACT.Copy).then_inc(s["wc_rdy"], 1)
            sqrt_var(0)
            def attention(g):
                act.wait_ge(s["xn_turned"], g + 1)
                act.activation(xnt[:, :], TP[:, :], ACT.Copy).then_inc(s["xnt_rdy"], 1)
                act.wait_ge(s["ctx_turned"], g + 1)
                act.activation(ctx_t[:, :, :], PK[:, 0:GB * M].rearrange("p (b m) -> p b m", b=GB),
                               ACT.Copy).then_inc(s["ctx_rdy"], 1)
                act.wait_ge(s["k1_mm"], g + 1)
                act.activation(k1_all[:, bass.ts(g, GB * M)], PQ[:, 0:GB * M], ACT.Identity,
                               bias=bcol[:, 1:2]).then_inc(s["k1_rdy"], 1)

                def exps(u):
                    for gg in range(HG):
                        act.wait_ge(s["st_mm"], (g * GB + u) * HG + gg + 1)
                        act.activation(prob[:, gg, :], SB[gg][0:M, :], ACT.Exp,
                                       scale=SCALE).then_inc(s["exp_rdy"], 1)

                def heads_out(u):
                    act.wait_ge(s["pv_mm"], g * GB + u + 1)
                    act.activation(ot[:, :], PO[:, 0:2 * P], ACT.Copy).then_inc(s["ot_rdy"], 1)

                def attn_t(u):
                    act.wait_ge(s["on_turned"], g * GB + u + 1)
                    act.activation(ont[:, :], TP[:, 0:P], ACT.Copy).then_inc(s["ont_rdy"], 1)

                for u in range(-1, GB):
                    if u >= 0:
                        heads_out(u)
                    if u + 1 < GB:
                        exps(u + 1)
                    if u >= 0:
                        attn_t(u)

            steps(act, attention)
            act.wait_ge(s["xn_rdy"], G)
            act.wait_ge(s["xr_rdy"], 1)
            act.dma_start(w2_sb[:, :, :], a["L0_ffn_w2"].rearrange("e i h -> i e h")).then_inc(s["ld_w2"], 16)
            sqrt_var(1)
            act.wait_ge(s["wd_turned"], 1)
            act.activation(wdn[:, :, :], PK[:, :].rearrange("p (c d) -> p c d", c=HC), ACT.Copy).then_inc(s["wd_rdy"], 1)
            act.wait_ge(s["ub_turned"], 1)
            act.activation(upb[:, :], PQ[:, 0:HC], ACT.Copy).then_inc(s["upb_rdy"], 1)
            act.wait_ge(s["upb_rdy"], 1)
            sqrt_var(2)

            def attn1_xt(g):
                act.wait_ge(s["c_turned"], g + 1)
                act.activation(xct, TP[:, :], ACT.Copy).then_inc(s["c_xnt"], 1)

            def attn1_qt(g):
                act.wait_ge(s["c_q"], g + 1)
                act.activation(qt, TP[:, :], ACT.Identity, bias=bcol[:, 0:1]).then_inc(s["c_qt"], 1)

            def attn1_exp(g):
                act.wait_ge(s["c_max"], g + 1)
                for u in range(GB):
                    act.activation(p1[:, u, :], TP[:, u * M:(u + 1) * M], ACT.Exp, bias=mx1[:, u:u + 1],
                                   accum_out=sm1[:, u:u + 1]).then_inc(s["c_exp"], 1)

            def attn1_pt(g):
                act.wait_ge(s["c_p_turned"], g + 1)
                act.activation(p1t, TP[0:M, :], ACT.Copy).then_inc(s["c_pt"], 1)

            def normed_t(g):
                act.wait_ge(s["m_turned"], g + 1)
                need(act, "m_xl", g)
                act.activation(xnt[:, :], TP[:, :], ACT.Copy, scale=bcol[:, 2:3]).then_inc(s["m_xnt"], 1)
                act.wait_ge(s["m_xnt"], g + 1)
                act.activation(high(g), xnt[:, :], ACT.Copy).then_inc(s["m_xh"], 1)

            def router_exp(g):
                act.wait_ge(s["m_lgd"], g + 1)
                act.activation(gw[:, 1, :, :], gw[:, 0, :, :], ACT.Exp).then_inc(s["m_exp"], 1)

            def gates_t(g):
                act.wait_ge(s["m_g_turned"], g + 1)
                need(act, "m_gb", g * E)
                act.activation(gt[:, :], TP[0:2 * E, :], ACT.Copy).then_inc(s["m_gt"], 1)

            def mixed(g):
                act.wait_ge(s["m_y"], g * E + E)
                act.activation(ys, SB[0][:, :], ACT.Copy).then_inc(s["m_ys"], 1)

            def mixture(g):
                for e in range(E):
                    n = g * E + e + 1
                    act.wait_ge(s["m_ha"], n)
                    need(act, "m_s", n - 2)
                    act.activation(ea[:, e % 2, :], SB[1 + e % 2][:, :], ACT.Identity,
                                   bias=b1c[:, 0, e:e + 1]).then_inc(s["m_a"], 1)
                    need(act, "m_eq", n - 2)
                    act.activation(esg[:, e % 2, :], SB[1 + e % 2][:, :], ACT.Sigmoid, scale=ALPHA,
                                   bias=b1c[:, 2, e:e + 1]).then_inc(s["m_sg"], 1)
                    act.wait_ge(s["m_hb"], n)
                    need(act, "m_ec", n - 2)
                    act.activation(eb[:, e % 2, :], (SB[3], PK)[e % 2][:, :], ACT.Identity,
                                   bias=b1c[:, 1, e:e + 1]).then_inc(s["m_eb"], 1)
                    if e == LAG - 1 and not first(g):
                        mixed(g - 1)
                    if e == XT_AT and not last(g):
                        normed_t(g + 1)
                    if e == CX_AT and not first(g):
                        attn1_xt(g - 1)
                    if e == CQ_AT and not first(g):
                        attn1_qt(g - 1)
                    if e == EXP_AT and not last(g):
                        router_exp(g + 1)
                    if e == EXP_AT and not first(g):
                        attn1_exp(g - 1)
                    if e == CP_AT and not first(g):
                        attn1_pt(g - 1)
                    if e == E - 1 and not last(g):
                        gates_t(g + 1)

            normed_t(0)
            router_exp(0)
            gates_t(0)
            pipelined(act, mixture)
            mixed(G - 1)

            def hidden_xt(g):
                act.wait_ge(s["d_turned"], g + 1)
                act.activation(xnt[:, :], PK[:, :], ACT.Copy).then_inc(s["d_xnt"], 1)

            def hidden(g):
                if g >= 1:
                    act.wait_ge(s["d_o"], g)
                for c in range(HC):
                    act.wait_ge(s["d_h"], g * HC + c + 1)
                    act.activation(gh[:, c, :], SB[c][:, :], ACT.Gelu, bias=upb[:, c:c + 1]).then_inc(s["d_g"], 1)

            hidden_xt(0)
            attn1_xt(G - 1)
            hidden(0)
            attn1_qt(G - 1)
            hidden_xt(1)
            attn1_exp(G - 1)
            attn1_pt(G - 1)
            hidden(1)
            hidden_xt(2)
            hidden(2)
            hidden_xt(3)
            hidden(3)

        @block.tensor
        def _(pe):
            pe.wait_ge(s["consts"], 1)
            pe.wait_ge(s["ld_w"], 16 * NW)
            for i in range(NW):
                mm = pe.transpose((SB[0] if i < 4 else SB[1])[:, (i % 4) * P:(i % 4 + 1) * P], wnat[:, i, :],
                                  ident[:, :])
            mm.then_inc(s["w_turned"], 1)
            pe.wait_ge(s["bst_rdy"], 1)
            for j in range(2):
                for r in range(HR):
                    mm = pe.matmul(SB[2][:, j * HR + r:j * HR + r + 1], bst[:, j, r * P:(r + 1) * P],
                                   ident[0:1, 0:1], start=True, stop=True)
            mm.then_inc(s["bst_turned"], 1)
            pe.wait_ge(s["ld_moe"], 16 * 6)
            for j in range(2):
                mm = pe.transpose(SB[3][:, j * E:(j + 1) * E], b1_nat[:, j:2 * P:2], ident[0:E, 0:E])
            mm.then_inc(s["b1_turned"], 1)
            pe.wait_ge(s["ld_ffn"], 16 * 4)
            for c in range(HC):
                mm = pe.transpose(PK[:, c * P:(c + 1) * P], wcon[:, c, :], ident[:, :])
            mm.then_inc(s["wc_turned"], 1)
            pe.wait_ge(s["w_rdy"], 1)
            pe.wait_ge(s["b1_rdy"], 1)
            pe.wait_ge(s["wc_rdy"], 1)
            pe.wait_ge(s["pick_rdy"], 1)

            def attention(g):
                pe.wait_ge(s["xn_rdy"], g + 1)
                need(pe, "x1_rdy", g * GB)
                for u in range(GB):
                    mm = pe.transpose(TP[:, u * P:(u + 1) * P], xn[:, u, :], ident[:, :])
                mm.then_inc(s["xn_turned"], 1)
                pe.wait_ge(s["ctx_ld"], 16 * g + 16)
                need(pe, "kx_rdy", g * GB)
                for u in range(GB):
                    mm = pe.transpose(PK[:, u * M:(u + 1) * M], ctx_in[:, u, :], ident[0:M, 0:M])
                mm.then_inc(s["ctx_turned"], 1)
                pe.wait_ge(s["ctx_rdy"], g + 1)
                need(pe, "on_rdy", g * GB)
                for u in range(GB):
                    mm = pe.matmul(PO[0:M, u * P:(u + 1) * P], ctx_t[:, u, :], wt[:, WV0, :], start=True, stop=True)
                mm.then_inc(s["v0_mm"], 1)
                need(pe, "qx_rdy", g * GB)
                pe.matmul(PQ[:, 0:GB * M], wt[:, WK1, :], ctx_t[:, :, :], start=True, stop=True).then_inc(s["k1_mm"], 1)
                pe.wait_ge(s["xnt_rdy"], g + 1)
                for u in range(GB):
                    mm = pe.matmul(TP[0:M, u * P:(u + 1) * P], ctx_t[:, u, :], wt[:, WV1, :], start=True, stop=True)
                mm.then_inc(s["v1_mm"], 1)

                def k_stack(u):
                    if u >= 1:
                        pe.wait_ge(s["kx_rdy"], g * GB + u)
                    for r in range(HR):
                        mm = pe.matmul(PK[:, r * M:(r + 1) * M], wk_st[:, r, :, :], ctx_t[:, u, :],
                                       start=True, stop=True)
                    mm.then_inc(s["k_mm"], 1)

                def q_stack(u):
                    if u >= 1:
                        pe.wait_ge(s["qx_rdy"], g * GB + u)
                    else:
                        pe.wait_ge(s["k1_rdy"], g + 1)
                    for r in range(HR):
                        mm = pe.matmul(PQ[:, r * P:(r + 1) * P], wq_st[:, r, :, :], xnt[:, u * P:(u + 1) * P],
                                       start=True, stop=True)
                    mm.then_inc(s["q_mm"], 1)

                def scores(u):
                    pe.wait_ge(s["kx_rdy"], g * GB + u + 1)
                    pe.wait_ge(s["qx_rdy"], g * GB + u + 1)
                    for gg in range(HG):
                        need(pe, "exp_rdy", (g * GB + u - 1) * HG + gg + 1 if u >= 1 else g * GB * HG)
                        p0 = 32 * gg
                        for r in range(HR):
                            mm = pe.matmul(SB[gg][:, r * M:(r + 1) * M], qs[p0:p0 + 32, u % 2, r, :],
                                           ks[p0:p0 + 32, u % 2, r, :], start=True, stop=True)
                        mm.then_inc(s["s_mm"], 1)

                def turn_max(u):
                    pe.wait_ge(s["nt_rdy"], (g * GB + u + 1) * HG)
                    if u == 0:
                        pe.wait_ge(s["v1_rdy"], g + 1)
                    elif u == 1:
                        need(pe, "x1_rdy", g * GB)
                    else:
                        pe.wait_ge(s["x1_rdy"], g * GB + u - 1)
                    pe.transpose(TP[:, 0:P], nt[:, :, :].rearrange("p g c -> p (g c)"), ident[:, :]).then_inc(s["nt_turned"], 1)

                def scores_t(u):
                    pe.wait_ge(s["ntq_rdy"], g * GB + u + 1)
                    for gg in range(HG):
                        p0 = 32 * gg
                        for r in range(HR):
                            mm = pe.matmul(SB[gg][0:M, r * P:(r + 1) * P], ks[p0:p0 + 32, u % 2, r, :],
                                           qs[p0:p0 + 32, u % 2, r, :], start=True, stop=True)
                        mm.then_inc(s["st_mm"], 1)

                def values(u):
                    pe.wait_ge(s["exp_rdy"], (g * GB + u + 1) * HG)
                    if u == 0:
                        pe.wait_ge(s["v0_rdy"], g + 1)
                    else:
                        pe.wait_ge(s["on_rdy"], g * GB + u)
                    for h in range(H):
                        gg, r, j = h % HG, h // HG, (h % 8) // 2
                        mm = pe.matmul(PO[32 * j:32 * j + 32, (h // 8) * P:(h // 8 + 1) * P], vst[:, u, h, :],
                                       prob[:, gg, r * P:(r + 1) * P], start=(h % 2 == 0), stop=(h % 2 == 1))
                    mm.then_inc(s["pv_mm"], 1)

                def turn_heads(u):
                    pe.wait_ge(s["ot_rdy"], g * GB + u + 1)
                    for half in range(2):
                        mm = pe.transpose(PO[:, (2 + half) * P:(3 + half) * P], ot[:, half * P:(half + 1) * P],
                                          ident[:, :])
                    mm.then_inc(s["ot_turned"], 1)

                def turn_attn(u):
                    pe.wait_ge(s["on_rdy"], g * GB + u + 1)
                    if u + 1 < GB:
                        pe.wait_ge(s["ntq_rdy"], g * GB + u + 2)
                    pe.transpose(TP[:, 0:P], on[:, :, :].rearrange("p h d -> p (h d)"), ident[:, :]).then_inc(s["on_turned"], 1)

                def project(u):
                    pe.wait_ge(s["ont_rdy"], g * GB + u + 1)
                    pe.matmul(TP[:, P:2 * P], ont[:, :], wt[:, WO0, :], start=True, stop=True).then_inc(s["o_mm"], 1)

                k_stack(0)
                q_stack(0)
                for u in range(-1, GB):
                    if u + 1 < GB:
                        scores(u + 1)
                    if u >= 1:
                        project(u - 1)
                    if u >= 0:
                        values(u)
                    if u + 2 < GB:
                        k_stack(u + 2)
                    if u + 1 < GB:
                        turn_max(u + 1)
                    if u + 2 < GB:
                        q_stack(u + 2)
                    if u >= 0:
                        turn_heads(u)
                    if u + 1 < GB:
                        scores_t(u + 1)
                    if u >= 0:
                        turn_attn(u)
                project(GB - 1)

            steps(pe, attention)

            pe.wait_ge(s["w1_split"], E // 4)
            pe.wait_ge(s["ld_w2"], 16)
            HA, HB_, GBK, Y = SB[1:3], (SB[3], PK), (PQ, PO), SB[0]
            pe.wait_ge(s["x1_rdy"], G * GB)
            pe.wait_ge(s["bf_rdy"], 1)
            for c in range(HC):
                mm = pe.transpose(PK[:, c * P:(c + 1) * P], bfly[:, STAGES % 2, c * P:(c + 1) * P], ident[:, :])
            mm.then_inc(s["wd_turned"], 1)
            pe.wait_ge(s["ub_rdy"], 1)
            for c in range(HC):
                mm = pe.matmul(PQ[:, c:c + 1], ubias[:, c * P:(c + 1) * P], ident[0:1, 0:1], start=True, stop=True)
            mm.then_inc(s["ub_turned"], 1)
            pe.wait_ge(s["wd_rdy"], 1)
            pe.wait_ge(s["upb_rdy"], 1)
            def turn_normed(g):
                pe.wait_ge(s["m_xn"], g + 1)
                need(pe, "m_x2", g - 1)
                for u in range(GB):
                    mm = pe.transpose(TP[:, u * P:(u + 1) * P], xn[:, u, :], ident[:, :])
                mm.then_inc(s["m_turned"], 1)

            def logits(g):
                pe.wait_ge(s["m_xnt"], g + 1)
                for u in range(GB):
                    mm = pe.matmul(TP[:, u * E:(u + 1) * E], xnt[:, u * P:(u + 1) * P], wg_sb[:, :],
                                   start=True, stop=True)
                mm.then_inc(s["m_lg_mm"], 1)

            def turn_gates(g):
                pe.wait_ge(s["m_ghl"], g + 1)
                need(pe, "c_x3", g - 1)
                for u in range(GB):
                    mm = pe.transpose(TP[0:2 * E, u * P:(u + 1) * P], ghl[:, u, :], ident[:, :])
                mm.then_inc(s["m_g_turned"], 1)

            def up(g, e):
                n = g * E + e + 1
                for branch, bk, read, done in ((0, HA[e % 2], "m_sg", "m_ha"), (1, HB_[e % 2], "m_eb", "m_hb")):
                    need(pe, read, n - 2)
                    pe.matmul(bk[:, :], w1_hi[:, e, branch, :], low(g), start=True, stop=False)
                    pe.matmul(bk[:, :], w1_lo[:, e, branch, :], high(g), start=False, stop=False)
                    pe.matmul(bk[:, :], w1_hi[:, e, branch, :], high(g), start=False, stop=True).then_inc(s[done], 1)

            def gate(g, e):
                need(pe, "m_eq", g * E + e - 1)
                pe.matmul(GBK[e % 2][:, :], pick_e[:, e, :], gt[:, :], start=True, stop=True).then_inc(s["m_gb"], 1)

            def down(g, e):
                if e == 0:
                    need(pe, "m_ys", g)
                    pe.matmul(Y[:, :], b2_sb[:, :], gt[:, :].bitcast(F32), start=True, stop=False,
                              skip_group_check=True)
                pe.wait_ge(s["m_s"], g * E + e + 1)
                pe.matmul(Y[:, :], w2_sb[:, e, :], es[e % len(es)], start=False, stop=(e == E - 1),
                          skip_group_check=True).then_inc(s["m_y"], 1)

            def turn_mixed(g):
                pe.wait_ge(s["m_ys"], g + 1)
                for u in range(GB):
                    mm = pe.transpose(TP[:, u * P:(u + 1) * P], ys[:, u * P:(u + 1) * P], ident[:, :])
                mm.then_inc(s["m_ys_turned"], 1)

            def attn1_turn(g):
                pe.wait_ge(s["c_xn"], g + 1)
                pe.wait_ge(s["m_x2"], g + 1)
                pe.wait_ge(s["m_lgd"], min(g + 3, G) if isinstance(g, int) else g + 3)
                for u in range(GB):
                    mm = pe.transpose(TP[:, u * P:(u + 1) * P], xc[:, u, :], ident[:, :])
                mm.then_inc(s["c_turned"], 1)

            def attn1_q(g):
                pe.wait_ge(s["c_xnt"], g + 1)
                pe.matmul(TP[:, :], wt[:, WQ1, :], xct, start=True, stop=True).then_inc(s["c_q"], 1)

            def attn1_scores(g):
                pe.wait_ge(s["c_qt"], g + 1)
                for u in range(GB):
                    mm = pe.matmul(TP[:, u * M:(u + 1) * M], qt[:, u * P:(u + 1) * P],
                                   k1_all[:, bass.ds((g * GB + u) * M, M)], start=True, stop=True)
                mm.then_inc(s["c_s"], 1)

            def attn1_p(g):
                pe.wait_ge(s["c_exp"], (g + 1) * GB)
                for u in range(GB):
                    mm = pe.transpose(TP[0:M, u * P:(u + 1) * P], p1[:, u, :], ident[:, :])
                mm.then_inc(s["c_p_turned"], 1)

            def attn1_values(g):
                pe.wait_ge(s["c_pt"], g + 1)
                for u in range(GB):
                    mm = pe.matmul(TP[:, u * P:(u + 1) * P], p1t[:, u * P:(u + 1) * P],
                                   v1_all[:, bass.ds(g * GB + u, 1), :], start=True, stop=True)
                mm.then_inc(s["c_pv"], 1)

            def mixture(g):
                pe.wait_ge(s["m_xl"], g + 1)
                for e in range(E):
                    up(g, e)
                    if e == 0:
                        pe.wait_ge(s["m_gt"], g + 1)
                    gate(g, e)
                    if e == LAG and not first(g):
                        turn_mixed(g - 1)
                    if e == XT_AT and not last(g):
                        turn_normed(g + 1)
                    if e == LG_AT and not last(g):
                        logits(g + 1)
                    if e == CX_AT and not first(g):
                        attn1_turn(g - 1)
                    if e == CQ_AT and not first(g):
                        attn1_q(g - 1)
                    if e == CS_AT and not first(g):
                        attn1_scores(g - 1)
                    if e == CP_AT and not first(g):
                        attn1_p(g - 1)
                    if e == CV_AT and not first(g):
                        attn1_values(g - 1)
                    if e == GT_AT and not last(g):
                        turn_gates(g + 1)
                    if e >= LAG:
                        down(g, e - LAG)
                    elif not first(g):
                        down(g - 1, E - LAG + e)

            turn_normed(0)
            logits(0)
            turn_gates(0)
            pipelined(pe, mixture)
            for e in range(E - LAG, E):
                down(G - 1, e)
            pe.wait_ge(s["c_x3"], G - 1)
            turn_mixed(G - 1)

            def turn_rows(g):
                pe.wait_ge(s["d_xn"], g + 1)
                if g >= 1:
                    pe.wait_ge(s["d_xnt"], g)
                for u in range(GB):
                    mm = pe.transpose(PK[:, u * P:(u + 1) * P], xn[:, u, :], ident[:, :])
                mm.then_inc(s["d_turned"], 1)

            def hidden_in(g):
                pe.wait_ge(s["d_xnt"], g + 1)
                for c in range(HC):
                    if g >= 1:
                        pe.wait_ge(s["d_g"], (g - 1) * HC + c + 1)
                    pe.matmul(SB[c][:, :], wup[:, c * P:(c + 1) * P], xnt[:, :], start=True,
                              stop=True).then_inc(s["d_h"], 1)

            def hidden_out(g):
                pe.wait_ge(s["d_g"], (g + 1) * HC)
                if g >= 1:
                    pe.wait_ge(s["d_x4"], g)
                for u in range(GB):
                    for c in range(HC):
                        mm = pe.matmul(PO[:, u * P:(u + 1) * P], gh[:, c, u * P:(u + 1) * P], wdn[:, c, :],
                                       start=(c == 0), stop=(c == HC - 1))
                mm.then_inc(s["d_o"], 1)

            turn_rows(0)
            hidden_in(0)
            attn1_turn(G - 1)
            attn1_q(G - 1)
            turn_rows(1)
            attn1_scores(G - 1)
            hidden_in(1)
            attn1_p(G - 1)
            attn1_values(G - 1)
            hidden_out(0)
            turn_rows(2)
            hidden_in(2)
            hidden_out(1)
            turn_rows(3)
            hidden_in(3)
            hidden_out(2)
            hidden_out(3)

        @block.vector
        def _(dve):
            own = Own(dve, s["dve_own"])
            dve.wait_ge(s["consts"], 1)
            dve.tensor_copy(pick_e[:, :, :], pick_e_raw[:, :, :]).then_inc(s["pick_rdy"], 1)
            dve.wait_ge(s["ld_small"], 16 * 11)
            for j in range(2):
                ins = dve.tensor_copy(bst[:, j, :].rearrange("o (h c) -> o h c", c=32)[:, :, 0:HD],
                                      brow[:, j, :].rearrange("o (h d) -> o h d", d=HD))
            ins.then_inc(s["bst_rdy"], 1)
            dve.wait_ge(s["bst_turned"], 1)
            dve.tensor_copy(bst_c[:, :, :], SB[2][:, 0:2 * HR].rearrange("p (j r) -> p j r", j=2)
                            ).then_inc(s["bst_c_rdy"], 1)
            dve.wait_ge(s["bst_c_rdy"], 1)
            dve.wait_ge(s["w_turned"], 1)
            dve.tensor_copy(wt[:, 0:4, :], SB[0][:, :].rearrange("p (i c) -> p i c", i=4))
            dve.tensor_copy(wt[:, 4:NW, :], SB[1][:, 0:(NW - 4) * P].rearrange("p (i c) -> p i c", i=NW - 4))
            for i, dst in ((WQ0, wq_st), (WK0, wk_st)):
                src = SB[0][:, i * P:(i + 1) * P].rearrange("p (h d) -> p h d", d=HD)
                o = dst[:, :, :, :].rearrange("p r g c -> p (r g) c")
                ins = dve.tensor_copy(o[:, :, 0:HD], src)
            ins.then_inc(s["w_rdy"], 1)
            dve.wait_ge(s["b1_turned"], 1)
            own.mark(dve.tensor_copy(b1c[:, 0, :], SB[3][:, 0:E]))
            own.mark(dve.tensor_scalar(b1c[:, 1, :], SB[3][:, E:2 * E], 1.0, None, ALU.add))
            own.mark(dve.tensor_scalar(b1c[:, 2, :], SB[3][:, 0:E], ALPHA, None, ALU.mult))
            own.wait()
            dve.tensor_copy(st[:, 5, 0:1], b1c[:, 0, 0:1]).then_inc(s["b1_rdy"], 1)

            def rsqrt_steps(dst, n):
                dve.wait_ge(s["ln_sqrt"], n + 1)
                own.then_wait(dve.reciprocal(st[:, 3, :], st[:, 2, :]))
                own.then_wait(dve.tensor_tensor(st[:, 4, :], st[:, 3, :], st[:, 3, :], ALU.mult))
                own.then_wait(dve.tensor_tensor(st[:, 4, :], st[:, 4, :], st[:, 1, :], ALU.mult))
                own.then_wait(dve.tensor_scalar(st[:, 4, :], st[:, 4, :], -0.5, 1.5, ALU.mult, ALU.add))
                own.then_wait(dve.tensor_tensor(dst[:, :], st[:, 3, :], st[:, 4, :], ALU.mult))

            def layer_stats(n):
                own.mark(dve.tensor_tensor(mean[:, :], stats[:, :, 1], stats[:, :, 4], ALU.add))
                own.mark(dve.tensor_tensor(st[:, 0, :], stats[:, :, 1], stats[:, :, 4], ALU.subtract))
                own.mark(dve.tensor_tensor(st[:, 1, :], stats[:, :, 2], stats[:, :, 5], ALU.add))
                own.wait()
                own.mark(dve.tensor_scalar(mean[:, :], mean[:, :], 0.5, None, ALU.mult))
                own.mark(dve.tensor_tensor(st[:, 0, :], st[:, 0, :], st[:, 0, :], ALU.mult))
                own.mark(dve.tensor_scalar(st[:, 1, :], st[:, 1, :], 1.0 / D, EPS, ALU.mult, ALU.add))
                own.wait()
                dve.scalar_tensor_tensor(st[:, 1, :], st[:, 0, :], 0.25, st[:, 1, :], ALU.mult, ALU.add
                                         ).then_inc(s["ln_var"], 1)
                dve.wait_ge(s["ln_var"], n + 1)
                rsqrt_steps(rstd, n)

            dve.wait_ge(s["ld_x"], 16 * G)
            for b in range(NB):
                own.mark(dve.bn_stats(stats[:, b, :], x_sb[:, b, :]))
            own.wait()
            layer_stats(0)
            dve.wait_ge(s["xr_rdy"], 1)
            own.then_wait(dve.tensor_copy(st[:, 5, :], mean[:, :]))
            OWN_A, PER_A = own.base + own.n, 2 * GB
            def attention(g):
                own.base, own.n = OWN_A + g * PER_A, 0
                for u in range(GB):
                    b = bass.ds(g * GB + u, 1)
                    ins = dve.tensor_scalar(xn[:, u, :], x_sb[:, b, :].rearrange("p o d -> p (o d)"),
                                            mean[:, b], rstd[:, b], ALU.subtract, ALU.mult)
                ins.then_inc(s["xn_rdy"], 1)
                dve.wait_ge(s["v0_mm"], g + 1)
                for i in range(2):
                    ins = dve.tensor_tensor(
                        vst[:, :, :, :].rearrange("p b (x i) c -> p b x i c", i=2)[:, :, :, i, 16 * i:16 * i + HD],
                        PO[0:M, :].rearrange("p (b x i d) -> p b x i d", b=GB, x=H // 2, i=2)[:, :, :, i, :],
                        bcast[0:M, BV0, :].rearrange("p (x i d) -> p x i d", x=H // 2, i=2)[:, :, i, :]
                        .unsqueeze(1).to_broadcast([M, GB, H // 2, HD]), ALU.add)
                ins.then_inc(s["v0_rdy"], 1)
                dve.wait_ge(s["v1_mm"], g + 1)
                dve.tensor_tensor(v1_all[:, bass.ts(g, GB), :],
                                  TP[0:M, :].rearrange("p (b d) -> p b d", b=GB),
                                  bcast[0:M, BV1, :].unsqueeze(1).to_broadcast([M, GB, D]),
                                  ALU.add).then_inc(s["v1_rdy"], 1)

                def k_stacked(u):
                    dve.wait_ge(s["k_mm"], g * GB + u + 1)
                    dve.tensor_tensor(ks[:, u % 2, :, :], PK[:, 0:HR * M].rearrange("p (r m) -> p r m", r=HR),
                                      bst_c[:, 1, :].unsqueeze(2).to_broadcast([P, HR, M]), ALU.add
                                      ).then_inc(s["kx_rdy"], 1)

                def q_stacked(u):
                    dve.wait_ge(s["q_mm"], g * GB + u + 1)
                    dve.tensor_tensor(qs[:, u % 2, :, :], PQ[:, :].rearrange("p (r m) -> p r m", r=HR),
                                      bst_c[:, 0, :].unsqueeze(2).to_broadcast([P, HR, P]), ALU.add
                                      ).then_inc(s["qx_rdy"], 1)

                def maxima(u):
                    for gg in range(HG):
                        dve.wait_ge(s["s_mm"], (g * GB + u) * HG + gg + 1)
                        dve.tensor_reduce(nt[:, gg, HD:HD + HR], SB[gg][:, 0:HR * M].rearrange("p (r m) -> p r m", r=HR),
                                          AX.X, ALU.max, negate=True).then_inc(s["nt_rdy"], 1)

                def add_maxima(u):
                    dve.wait_ge(s["nt_turned"], g * GB + u + 1)
                    q = qs[:, u % 2, :, :]
                    dve.tensor_tensor(q, q, TP[:, 0:P].unsqueeze(1).to_broadcast([P, HR, P]), ALU.add
                                      ).then_inc(s["ntq_rdy"], 1)

                def weighted(u):
                    dve.wait_ge(s["ot_turned"], g * GB + u + 1)
                    pv = PO[:, 2 * P:4 * P].rearrange("p (h c) -> p h c", h=H)
                    own.then_wait(dve.reciprocal(rden[:, :], pv[:, :, HD]))
                    dve.tensor_tensor(on[:, :, :], pv[:, :, 0:HD], rden[:, :].unsqueeze(2).to_broadcast([P, H, HD]),
                                      ALU.mult).then_inc(s["on_rdy"], 1)

                def residual(u):
                    dve.wait_ge(s["o_mm"], g * GB + u + 1)
                    b = bass.ds(g * GB + u, 1)
                    row = xr[:, b, :].rearrange("p o d -> p (o d)")
                    dve.scalar_tensor_tensor(row, TP[:, P:2 * P], tg[:, 0:1], row,
                                             ALU.mult, ALU.add).then_inc(s["x1_rdy"], 1)
                    dve.wait_ge(s["x1_rdy"], g * GB + u + 1)
                    own.mark(dve.bn_stats(stats[:, b, :].rearrange("p o s -> p (o s)"), row))

                k_stacked(0)
                q_stacked(0)
                for u in range(-1, GB):
                    if u + 1 < GB:
                        maxima(u + 1)
                    if u >= 1:
                        residual(u - 1)
                    if u + 2 < GB:
                        k_stacked(u + 2)
                    if u + 1 < GB:
                        add_maxima(u + 1)
                    if u + 2 < GB:
                        q_stacked(u + 2)
                    if u >= 0:
                        weighted(u)
                residual(GB - 1)
                assert own.n == PER_A

            steps(dve, attention)
            own.base, own.n = OWN_A + G * PER_A, 0
            own.wait()
            layer_stats(1)

            own.then_wait(dve.tensor_tensor(st[:, 0, :], rstd[:, :], rstd[:, :], ALU.mult))
            own.then_wait(dve.tensor_scalar(st[:, 3, :], st[:, 1, :], -EPS, None, ALU.add))
            own.then_wait(dve.tensor_tensor(st[:, 0, :], st[:, 0, :], st[:, 3, :], ALU.mult))
            dve.tensor_scalar(st[:, 1, :], st[:, 0, :], EPS, None, ALU.add).then_inc(s["ln_var"], 1)
            dve.wait_ge(s["ln_var"], 3)
            rsqrt_steps(rms, 2)
            own.then_wait(dve.tensor_tensor(rms[:, :], rms[:, :], rstd[:, :], ALU.mult))
            def norm_rows(g):
                for u in range(GB):
                    b = bass.ds(g * GB + u, 1)
                    ins = dve.tensor_scalar(xn[:, u, :], xr[:, b, :].rearrange("p o d -> p (o d)"),
                                            mean[:, b], rms[:, b], ALU.subtract, ALU.mult)
                ins.then_inc(s["m_xn"], 1)

            def router_top(g):
                dve.wait_ge(s["m_lg_mm"], g + 1)
                own.then_wait(dve.tensor_tensor(lg[:, :, :], TP[:, 0:GB * E].rearrange("p (b e) -> p b e", b=GB),
                                                bg_bc[:, :].unsqueeze(1).to_broadcast([P, GB, E]), ALU.add))
                dve.tensor_copy(gs[:, 3, 0:1], lg[:, 0, 0:1])
                for u in range(GB):
                    own.mark(dve.max(top[:, u, :], lg[:, u, :]))
                own.wait()
                best = top[:, :, 0:1].to_broadcast([P, GB, E])
                dve.tensor_tensor(gw[:, 0, :, :], lg[:, :, :], best, ALU.subtract).then_inc(s["m_lgd"], 1)

            def router_ties(g):
                fourth = top[:, :, 3:4].to_broadcast([P, GB, E])
                own.mark(dve.tensor_tensor(gw[:, 2, :, :], lg[:, :, :], fourth, ALU.is_gt))
                own.mark(dve.tensor_tensor(gw[:, 3, :, :], lg[:, :, :], fourth, ALU.is_equal))
                own.wait()
                own.mark(dve.tensor_reduce(gs[:, 0, :], gw[:, 2, :, :], AX.X, ALU.add))
                src = 3
                for k, step in enumerate((1, 2, 4, 8)):
                    dst = 4 + k % 2
                    own.mark(dve.tensor_copy(gw[:, dst, :, 0:step], gw[:, src, :, 0:step]))
                    own.mark(dve.tensor_tensor(gw[:, dst, :, step:E], gw[:, src, :, step:E],
                                               gw[:, src, :, 0:E - step], ALU.add))
                    own.wait()
                    src = dst

            def router_chosen(g):
                own.then_wait(dve.tensor_tensor(gw[:, 4, :, :], gw[:, 5, :, :],
                                                gs[:, 0, :].unsqueeze(2).to_broadcast([P, GB, E]), ALU.add))
                own.then_wait(dve.scalar_tensor_tensor(gw[:, 4, :, :], gw[:, 4, :, :], 4.5, gw[:, 3, :, :],
                                                       ALU.is_lt, ALU.mult))
                own.then_wait(dve.tensor_tensor(gw[:, 2, :, :], gw[:, 2, :, :], gw[:, 4, :, :], ALU.add))
                dve.wait_ge(s["m_exp"], g + 1)
                own.then_wait(dve.tensor_tensor(gw[:, 2, :, :], gw[:, 2, :, :], gw[:, 1, :, :], ALU.mult))

            def router_gates(g):
                own.then_wait(dve.tensor_reduce(gs[:, 1, :], gw[:, 2, :, :], AX.X, ALU.add))
                own.then_wait(dve.reciprocal(gs[:, 2, :], gs[:, 1, :]))
                own.then_wait(dve.tensor_tensor(gw[:, 2, :, :], gw[:, 2, :, :],
                                                gs[:, 2, :].unsqueeze(2).to_broadcast([P, GB, E]), ALU.mult))
                own.then_wait(dve.tensor_copy(ghr[:, :, :], gw[:, 2, :, :]))
                need(dve, "m_g_turned", g)
                dve.tensor_copy(ghl[:, :, 0:E], ghr[:, :, :].bitcast(F32))
                dve.tensor_tensor(ghl[:, :, E:2 * E], gw[:, 2, :, :], ghr[:, :, :].bitcast(F32),
                                  ALU.subtract).then_inc(s["m_ghl"], 1)

            def rows_again(g):
                for u in range(GB):
                    b = bass.ds(g * GB + u, 1)
                    own.mark(dve.tensor_scalar(xo[:, u, :], xr[:, b, :].rearrange("p o d -> p (o d)"),
                                               mean[:, b], rstd[:, b], ALU.subtract, ALU.mult))

            def residual2(g):
                own.wait()
                dve.wait_ge(s["m_ys_turned"], g + 1)
                own.then_wait(dve.tensor_tensor(xo[:, :, :], xo[:, :, :],
                                                TP[:, :].rearrange("p (b d) -> p b d", b=GB), ALU.add))
                rows = xr[:, bass.ts(g, GB), :]
                dve.scalar_tensor_tensor(rows, xo[:, :, :], tg[:, 2:3], rows, ALU.mult, ALU.add
                                         ).then_inc(s["m_x2"], 1)

            def row_stats(g):
                dve.wait_ge(s["m_x2"], g + 1)
                for u in range(GB):
                    b = bass.ds(g * GB + u, 1)
                    own.mark(dve.bn_stats(stats[:, b, :].rearrange("p o s -> p (o s)"),
                                          xr[:, b, :].rearrange("p o d -> p (o d)")))

            def variances(n, stat, mean_):
                own.mark(dve.tensor_tensor(mean_, stat[:, :, 1], stat[:, :, 4], ALU.add))
                own.mark(dve.tensor_tensor(cs[:, 2, 0:n], stat[:, :, 1], stat[:, :, 4], ALU.subtract))
                own.mark(dve.tensor_tensor(cs[:, 3, 0:n], stat[:, :, 2], stat[:, :, 5], ALU.add))
                own.wait()
                own.mark(dve.tensor_scalar(mean_, mean_, 0.5, None, ALU.mult))
                own.mark(dve.tensor_tensor(cs[:, 2, 0:n], cs[:, 2, 0:n], cs[:, 2, 0:n], ALU.mult))
                own.mark(dve.tensor_scalar(cs[:, 3, 0:n], cs[:, 3, 0:n], 1.0 / D, EPS, ALU.mult, ALU.add))
                own.wait()
                dve.scalar_tensor_tensor(cs[:, 0, 0:n], cs[:, 2, 0:n], 0.25, cs[:, 3, 0:n], ALU.mult, ALU.add
                                         ).then_inc(s["ln2_var"], 1)

            def refined(k, n, rstd_):
                dve.wait_ge(s["ln2_pow"], k)
                own.then_wait(dve.tensor_tensor(cs[:, 4, 0:n], cs[:, 1, 0:n], cs[:, 1, 0:n], ALU.mult))
                own.then_wait(dve.tensor_tensor(cs[:, 4, 0:n], cs[:, 4, 0:n], cs[:, 0, 0:n], ALU.mult))
                own.then_wait(dve.tensor_scalar(cs[:, 4, 0:n], cs[:, 4, 0:n], -0.5, 1.5, ALU.mult, ALU.add))
                own.then_wait(dve.tensor_tensor(rstd_, cs[:, 1, 0:n], cs[:, 4, 0:n], ALU.mult))

            def attn1_variances(g):
                dve.wait_ge(s["m_x2"], g + 1)
                dve.tensor_copy(gs[:, 3, 1:2], tg[:, 0:1])
                for u in range(GB):
                    b = bass.ds(g * GB + u, 1)
                    own.mark(dve.bn_stats(cst[:, u, :], xr[:, b, :].rearrange("p o d -> p (o d)")))
                own.wait()
                variances(GB, cst, cmean[:, :])

            def attn1_norm(g, k):
                refined(k, GB, crstd[:, :])
                for u in range(GB):
                    b = bass.ds(g * GB + u, 1)
                    ins = dve.tensor_scalar(xc[:, u, :], xr[:, b, :].rearrange("p o d -> p (o d)"),
                                            cmean[:, u:u + 1], crstd[:, u:u + 1], ALU.subtract, ALU.mult)
                ins.then_inc(s["c_xn"], 1)

            def attn1_maxima(g):
                dve.wait_ge(s["c_s"], g + 1)
                dve.tensor_reduce(mx1[:, :], TP[:, 0:GB * M].rearrange("p (b m) -> p b m", b=GB),
                                  AX.X, ALU.max, negate=True).then_inc(s["c_max"], 1)

            def attn1_sums(g):
                dve.wait_ge(s["c_exp"], (g + 1) * GB)
                own.then_wait(dve.reciprocal(rs1[:, 0, :], sm1[:, :]))
                own.mark(dve.tensor_scalar(rs1[:, 1, :], rs1[:, 0, :], tg[:, 1:2], None, ALU.mult))

            def attn1_residual(g):
                own.wait()
                dve.wait_ge(s["c_pv"], g + 1)
                for u in range(GB):
                    row = xr[:, bass.ds(g * GB + u, 1), :].rearrange("p o d -> p (o d)")
                    ins = dve.scalar_tensor_tensor(row, TP[:, u * P:(u + 1) * P], rs1[:, 1, u:u + 1], row,
                                                   ALU.mult, ALU.add)
                ins.then_inc(s["c_x3"], 1)

            def attn1_stats(g):
                dve.wait_ge(s["c_x3"], g + 1)
                dve.tensor_copy(gs[:, 3, 1:2], tg[:, 0:1])
                for u in range(GB):
                    b = bass.ds(g * GB + u, 1)
                    own.mark(dve.bn_stats(stats[:, b, :].rearrange("p o s -> p (o s)"),
                                          xr[:, b, :].rearrange("p o d -> p (o d)")))

            def mixture(g):
                for e in range(E):
                    j, n = e % 2, g * E + e + 1
                    dve.wait_ge(s["m_a"], n)
                    own.mark(dve.tensor_scalar(ea[:, j, :], ea[:, j, :], LIMIT, None, ALU.min))
                    dve.wait_ge(s["m_sg"], n)
                    dve.wait_ge(s["m_gb"], n)
                    dve.scalar_tensor_tensor(eq[:, j, :], esg[:, j, :], SIG_LIMIT, (PQ, PO)[j][:, :],
                                             ALU.min, ALU.mult).then_inc(s["m_eq"], 1)
                    dve.wait_ge(s["m_eb"], n)
                    own.mark(dve.tensor_scalar(eb[:, j, :], eb[:, j, :], LIMIT + 1.0, 1.0 - LIMIT, ALU.min, ALU.max))
                    dve.wait_ge(s["m_eq"], n)
                    own.wait()
                    need(dve, "m_s", n - 2)
                    dve.tensor_tensor(ec[:, j, :], eb[:, j, :], eq[:, j, :], ALU.mult).then_inc(s["m_ec"], 1)
                    if not first(g):
                        if e == LAG - 1:
                            rows_again(g - 1)
                        if e == LAG:
                            residual2(g - 1)
                        if e == LAG + 1:
                            attn1_variances(g - 1)
                        if e == LAG + 3:
                            attn1_norm(g - 1, g)
                        if e == CS_AT:
                            attn1_maxima(g - 1)
                        if e == CP_AT:
                            attn1_sums(g - 1)
                        if e == CV_AT:
                            attn1_residual(g - 1)
                        if e == E - 1:
                            attn1_stats(g - 1)
                    if not last(g):
                        if e == LAG:
                            norm_rows(g + 1)
                        if e == LG_AT:
                            router_top(g + 1)
                        if e == LG_AT + 1:
                            router_ties(g + 1)
                        if e == LG_AT + 4:
                            router_chosen(g + 1)
                        if e == LG_AT + 5:
                            router_gates(g + 1)

            norm_rows(0)
            router_top(0)
            router_ties(0)
            router_chosen(0)
            router_gates(0)
            mixture(0)
            OWN_B, PER_B = own.base + own.n, 81
            with dve.Fori(1, G - 1) as g:
                own.base, own.n = OWN_B + (g - 1) * PER_B, 0
                mixture(g)
                assert own.n == PER_B, own.n
            own.base, own.n = OWN_B + (G - 2) * PER_B, 0
            mixture(G - 1)

            def normed(g):
                own.wait()
                if g >= 1:
                    dve.wait_ge(s["d_turned"], g)
                for u in range(GB):
                    b = g * GB + u
                    ins = dve.tensor_scalar(xn[:, u, :], xr[:, b, :], mean[:, b:b + 1], rstd[:, b:b + 1],
                                            ALU.subtract, ALU.mult)
                ins.then_inc(s["d_xn"], 1)

            def with_biases(g):
                dve.wait_ge(s["d_xn"], g + 1)
                rows = xr[:, g * GB:(g + 1) * GB, :]
                own.mark(dve.tensor_tensor(rows, rows, bcd[:, :].unsqueeze(1).to_broadcast([P, GB, D]), ALU.add))

            def residual4(g):
                rows = xr[:, g * GB:(g + 1) * GB, :]
                own.wait()
                dve.wait_ge(s["d_o"], g + 1)
                dve.scalar_tensor_tensor(rows, PO[:, :].rearrange("p (b d) -> p b d", b=GB), tg[:, 3:4], rows,
                                         ALU.mult, ALU.add).then_inc(s["d_x4"], 1)

            done = 3 * GB
            rows_again(G - 1)
            own.wait()
            variances(done, stats[:, 0:done, :], mean[:, 0:done])
            refined(G, done, rstd[:, 0:done])
            normed(0)
            residual2(G - 1)
            attn1_variances(G - 1)
            attn1_norm(G - 1, G + 1)
            normed(1)
            with_biases(0)
            attn1_maxima(G - 1)
            with_biases(1)
            attn1_sums(G - 1)
            attn1_residual(G - 1)
            residual4(0)
            normed(2)
            attn1_stats(G - 1)
            own.wait()
            variances(GB, stats[:, done:NB, :], mean[:, done:NB])
            refined(G + 2, GB, rstd[:, done:NB])
            normed(3)
            with_biases(2)
            with_biases(3)
            residual4(1)
            residual4(2)
            residual4(3)


_INS = ["x", "ctx_1024", "g_xattn", "g_ffn", "L0_xattn_Wq", "L0_xattn_bq", "L0_xattn_Wk", "L0_xattn_bk",
        "L0_xattn_Wv", "L0_xattn_bv", "L0_xattn_Wo", "L0_xattn_bo", "L0_ffn_norm_scale", "L0_ffn_wg",
        "L0_ffn_bg", "L0_ffn_w1", "L0_ffn_b1", "L0_ffn_w2", "L0_ffn_b2", "L1_xattn_Wq", "L1_xattn_bq",
        "L1_xattn_Wk", "L1_xattn_bk", "L1_xattn_Wv", "L1_xattn_bv", "L1_ffn_W_exp", "L1_ffn_b_exp",
        "L1_ffn_up_weights", "L1_ffn_up_bias", "L1_ffn_down_weights", "L1_ffn_W_con", "L1_ffn_b_con",
        "L1_ffn_down_bias"]


def kernel(**inputs):
    import concourse.bacc as bacc
    from concourse.bass_utils import run_bass_kernel_spmd

    nc = bacc.Bacc("TRN2", target_bir_lowering=False, num_devices=1)
    arrays, aps = {}, {}
    for name in _INS:
        v = np.ascontiguousarray(inputs[name])
        arrays[f"in_{name}"] = v
        aps[name] = nc.dram_tensor(f"in_{name}", v.shape, mybir.dt.from_np(v.dtype), kind="ExternalInput").ap()
    shape = arrays["in_x"].shape
    out = nc.dram_tensor("out", shape, F32, kind="ExternalOutput").ap()
    flamingo_layers(nc, aps, out)
    r = run_bass_kernel_spmd(nc, [arrays], core_ids=[0])
    return r.results[0]["out"]
```
